# Optimizing a Trainium2 kernel written in Bass

```python
import numpy as np
import jax
import jax.numpy as jnp

def _softmax(x, axis=-1):
    return jax.nn.softmax(x, axis=axis)

def _gelu(x):
    return jax.nn.gelu(x, approximate=True)

def _silu(x):
    return jax.nn.silu(x)

def _sigmoid(x):
    return jax.nn.sigmoid(x)

def _layernorm(x, axis=-1, eps=1e-05):
    m = jnp.mean(x, axis=axis, keepdims=True)
    v = jnp.var(x, axis=axis, keepdims=True)
    return (x - m) / jnp.sqrt(v + eps)

def _scatter_add(tgt, idx, src, axis=0):
    return tgt.at[idx].add(src)

def _segment_sum(src, seg, n):
    return jax.ops.segment_sum(src, seg, n)
kernel_name = 'mk_gnn_resnorm_d4_gnn_r32_6cab62'

def setup_inputs(seed: int=0):
    np.random.seed(seed)
    _w = jnp.asarray

    def _rec_inputs():
        import jax
        import jax.numpy as jnp
        _gk = jax.random.key(seed)
        x = 0.4998 + 0.2887 * jax.random.normal(jax.random.fold_in(_gk, 1), (3125, 16), jnp.float32)
        _s = jax.random.randint(jax.random.fold_in(_gk, 2), (50000,), 0, 3125, jnp.int32)
        _d = jax.random.randint(jax.random.fold_in(_gk, 3), (50000,), 0, 3125, jnp.int32)
        _loop = jnp.arange(3125, dtype=jnp.int32)
        src = jnp.concatenate([_s, _d, _loop])
        dst = jnp.concatenate([_d, _s, _loop])
        _o = jnp.argsort(dst, stable=True)
        src = src[_o]
        dst = dst[_o]
        edge_attr_16 = -0.00010739 + 0.99994 * jax.random.normal(jax.random.fold_in(_gk, 12), (103125, 16), jnp.float32)
        edge_type_8 = jax.random.randint(jax.random.fold_in(_gk, 14), (103125,), 0, 8, jnp.int32)
        edge_type_90 = jax.random.randint(jax.random.fold_in(_gk, 15), (103125,), 0, 90, jnp.int32)
        edge_weight = jax.random.uniform(jax.random.fold_in(_gk, 16), (103125,), jnp.float32, 0.0, 1)
        return (x, src, dst, edge_attr_16, edge_type_8, edge_type_90, edge_weight)
    x, src, dst, edge_attr_16, edge_type_8, edge_type_90, edge_weight = _rec_inputs()

    def _L0_gnn_setup():
        import jax, jax.numpy as jnp
        import numpy as np
        N_NODES = 3125
        key = jax.random.key(seed)
        k1, k2, k3, k4 = jax.random.split(key, 4)
        E = 100000
        D = 16
        x = jax.random.uniform(k1, (N_NODES, D), dtype=jnp.float32)
        edge_index = jax.random.randint(k2, (2, E), 0, N_NODES, dtype=jnp.int64)
        edge_probs = jax.random.uniform(k3, (E,), dtype=jnp.float32)
        weight = jnp.ones((D,), dtype=jnp.float32)
        self_loop_weight = jnp.asarray(0.1, dtype=jnp.float32)
        return {'x': x, 'edge_index': edge_index, 'edge_probs': edge_probs, 'weight': weight, 'self_loop_weight': self_loop_weight}
    _L0_gnn_all = _L0_gnn_setup()
    _L0_gnn_in = {k: v for k, v in _L0_gnn_all.items() if k in ('weight', 'self_loop_weight')}
    del _L0_gnn_all

    def _L1_gnn_setup():
        import jax, jax.numpy as jnp
        import numpy as np
        N_NODES = 15625
        N_EDGES = 156250
        D = 16
        key = jax.random.key(seed)
        k1, k2, k3, k4 = jax.random.split(key, 4)
        x = jax.random.normal(k1, (N_NODES, D), dtype=jnp.float32)
        edge_index = jax.random.randint(k2, (2, N_EDGES), 0, N_NODES, dtype=jnp.int32)
        scale = 1.0 / np.sqrt(D)
        W_l = jax.random.uniform(k3, (D, D), minval=-scale, maxval=scale, dtype=jnp.float32)
        b_l = jnp.zeros((D,), dtype=jnp.float32)
        W_r = jax.random.uniform(k4, (D, D), minval=-scale, maxval=scale, dtype=jnp.float32)
        return {'x': x, 'edge_index': edge_index, 'W_l': W_l, 'b_l': b_l, 'W_r': W_r}
    _L1_gnn_all = _L1_gnn_setup()
    _L1_gnn_in = {k: v for k, v in _L1_gnn_all.items() if k in ('W_l', 'b_l', 'W_r')}
    del _L1_gnn_all

    def _L2_gnn_setup():
        import jax, jax.numpy as jnp
        import numpy as np
        N_NODES = 3125
        N_EDGES = 31250
        MSG_DIM = 16
        HID_DIM = 16
        N_EDGE_TYPE = 8
        key = jax.random.key(seed)
        ks = jax.random.split(key, 9)
        features = jax.random.normal(ks[0], (N_NODES, HID_DIM), dtype=jnp.float32)
        edge_src = jax.random.randint(ks[1], (N_EDGES,), 0, N_NODES, dtype=jnp.int32)
        edge_dst = jax.random.randint(ks[2], (N_EDGES,), 0, N_NODES, dtype=jnp.int32)
        edge_type = jax.random.randint(ks[3], (N_EDGES,), 0, N_EDGE_TYPE, dtype=jnp.int32)
        edge_emb = jax.random.normal(ks[4], (N_EDGE_TYPE, MSG_DIM * HID_DIM), dtype=jnp.float32) * 0.1
        s = 1.0 / np.sqrt(HID_DIM)
        w_ih = jax.random.uniform(ks[5], (3 * HID_DIM, MSG_DIM), minval=-s, maxval=s, dtype=jnp.float32)
        w_hh = jax.random.uniform(ks[6], (3 * HID_DIM, HID_DIM), minval=-s, maxval=s, dtype=jnp.float32)
        b_ih = jax.random.uniform(ks[7], (3 * HID_DIM,), minval=-s, maxval=s, dtype=jnp.float32)
        b_hh = jax.random.uniform(ks[8], (3 * HID_DIM,), minval=-s, maxval=s, dtype=jnp.float32)
        return {'features': features, 'edge_src': edge_src, 'edge_dst': edge_dst, 'edge_type': edge_type, 'edge_emb': edge_emb, 'w_ih': w_ih, 'w_hh': w_hh, 'b_ih': b_ih, 'b_hh': b_hh}
    _L2_gnn_all = _L2_gnn_setup()
    _L2_gnn_in = {k: v for k, v in _L2_gnn_all.items() if k in ('edge_emb', 'w_ih', 'w_hh', 'b_ih', 'b_hh')}
    del _L2_gnn_all

    def _L3_gnn_setup():
        import jax, jax.numpy as jnp
        import numpy as np
        N, E, IN, OUT, R, B = (50000, 25000, 16, 16, 90, 30)
        key = jax.random.key(seed)
        ks = jax.random.split(key, 9)
        h = jax.random.normal(ks[0], (N, IN), dtype=jnp.float32)
        he = jax.random.normal(ks[1], (E, IN), dtype=jnp.float32)
        Ws = jax.random.normal(ks[2], (OUT, IN), dtype=jnp.float32) * 0.1
        Wa = jax.random.normal(ks[3], (1, 3 * OUT), dtype=jnp.float32) * 0.1
        weight = jax.random.normal(ks[4], (B, IN, OUT), dtype=jnp.float32) * 0.1
        w_comp = jax.random.normal(ks[5], (R, B), dtype=jnp.float32) * 0.1
        src = jax.random.randint(ks[6], (E,), 0, N)
        dst = jax.random.randint(ks[7], (E,), 0, N)
        rel_type = jax.random.randint(ks[8], (E,), 0, R)
        return {'h': h, 'he': he, 'Ws': Ws, 'Wa': Wa, 'weight': weight, 'w_comp': w_comp, 'src': src, 'dst': dst, 'rel_type': rel_type}
    _L3_gnn_all = _L3_gnn_setup()
    _L3_gnn_in = {k: v for k, v in _L3_gnn_all.items() if k in ('Ws', 'Wa', 'weight', 'w_comp')}
    del _L3_gnn_all
    return {'x': x, 'src': src, 'dst': dst, 'edge_attr_16': edge_attr_16, 'edge_type_8': edge_type_8, 'edge_type_90': edge_type_90, 'edge_weight': edge_weight, 'L0_gnn_weight': _L0_gnn_in['weight'], 'L0_gnn_self_loop_weight': _L0_gnn_in['self_loop_weight'], 'L1_gnn_W_l': _L1_gnn_in['W_l'], 'L1_gnn_b_l': _L1_gnn_in['b_l'], 'L1_gnn_W_r': _L1_gnn_in['W_r'], 'L2_gnn_edge_emb': _L2_gnn_in['edge_emb'], 'L2_gnn_w_ih': _L2_gnn_in['w_ih'], 'L2_gnn_w_hh': _L2_gnn_in['w_hh'], 'L2_gnn_b_ih': _L2_gnn_in['b_ih'], 'L2_gnn_b_hh': _L2_gnn_in['b_hh'], 'L3_gnn_Ws': _L3_gnn_in['Ws'], 'L3_gnn_Wa': _L3_gnn_in['Wa'], 'L3_gnn_weight': _L3_gnn_in['weight'], 'L3_gnn_w_comp': _L3_gnn_in['w_comp']}

def reference(x, src, dst, edge_attr_16, edge_type_8, edge_type_90, edge_weight, L0_gnn_weight, L0_gnn_self_loop_weight, L1_gnn_W_l, L1_gnn_b_l, L1_gnn_W_r, L2_gnn_edge_emb, L2_gnn_w_ih, L2_gnn_w_hh, L2_gnn_b_ih, L2_gnn_b_hh, L3_gnn_Ws, L3_gnn_Wa, L3_gnn_weight, L3_gnn_w_comp):
    import jax
    import jax.numpy as jnp

    def _L0_gnn_ref(x, edge_index, edge_probs, weight, self_loop_weight):
        import jax, jax.numpy as jnp
        import numpy as np
        N_NODES = 3125
        src = edge_index[0]
        dst = edge_index[1]
        messages = x[src] * edge_probs[:, None] * weight
        out = jax.ops.segment_sum(messages, dst, num_segments=N_NODES)
        out = out + x * self_loop_weight
        return jnp.clip(x + out, 0.0, 1.0)

    def _L1_gnn_ref(x, edge_index, W_l, b_l, W_r):
        import jax, jax.numpy as jnp
        import numpy as np
        N_NODES = 15625
        N_EDGES = 156250
        D = 16
        src = edge_index[0]
        dst = edge_index[1]
        n = x.shape[0]
        agg = jax.ops.segment_sum(x[src], dst, num_segments=n)
        cnt = jax.ops.segment_sum(jnp.ones((src.shape[0],), dtype=x.dtype), dst, num_segments=n)
        mean = agg / jnp.maximum(cnt, 1.0)[:, None]
        return mean @ W_l.T + b_l + x @ W_r.T

    def _L2_gnn_ref(features, edge_src, edge_dst, edge_type, edge_emb, w_ih, w_hh, b_ih, b_hh):
        import jax, jax.numpy as jnp
        import numpy as np
        N_NODES = 3125
        N_EDGES = 31250
        MSG_DIM = 16
        HID_DIM = 16
        N_EDGE_TYPE = 8
        n_nodes = features.shape[0]
        A = edge_emb[edge_type].reshape(-1, MSG_DIM, HID_DIM)
        h_src = features[edge_src]
        msg = jnp.einsum('emh,eh->em', A, h_src)
        m = jax.ops.segment_sum(msg, edge_dst, num_segments=n_nodes)
        gi = m @ w_ih.T + b_ih
        gh = features @ w_hh.T + b_hh
        i_r, i_z, i_n = jnp.split(gi, 3, axis=-1)
        h_r, h_z, h_n = jnp.split(gh, 3, axis=-1)
        r = jax.nn.sigmoid(i_r + h_r)
        z = jax.nn.sigmoid(i_z + h_z)
        n = jnp.tanh(i_n + r * h_n)
        h_new = (1.0 - z) * n + z * features
        return h_new

    def _L3_gnn_ref(h, he, Ws, Wa, weight, w_comp, src, dst, rel_type):
        import jax, jax.numpy as jnp
        import numpy as np
        N, E, IN, OUT, R, B = (50000, 25000, 16, 16, 90, 30)
        n_nodes, in_dim = h.shape
        num_bases, _, out_dim = weight.shape
        num_rels = w_comp.shape[0]
        V = weight.reshape(in_dim, num_bases, out_dim)
        W_rel = jnp.matmul(w_comp, V).reshape(num_rels, in_dim, out_dim)
        h_src = h[src]
        z_src = h_src @ Ws.T
        z_dst = h[dst] @ Ws.T
        z_e = he @ Ws.T
        e = jnp.concatenate([z_src, z_e, z_dst], axis=1) @ Wa.T
        msg = jnp.einsum('ei,eio->eo', h_src, W_rel[rel_type]) * e
        h_out = jax.ops.segment_sum(msg, dst, num_segments=n_nodes)
        return h_out
    edge_index = jnp.stack([src, dst])
    x = _layernorm(x + _L0_gnn_ref(x, edge_index, edge_weight, L0_gnn_weight, L0_gnn_self_loop_weight), axis=-1)
    x = _layernorm(x + _L1_gnn_ref(x, edge_index, L1_gnn_W_l, L1_gnn_b_l, L1_gnn_W_r), axis=-1)
    x = _layernorm(x + _L2_gnn_ref(x, src, dst, edge_type_8, L2_gnn_edge_emb, L2_gnn_w_ih, L2_gnn_w_hh, L2_gnn_b_ih, L2_gnn_b_hh), axis=-1)
    x = _layernorm(x + _L3_gnn_ref(x, edge_attr_16, L3_gnn_Ws, L3_gnn_Wa, L3_gnn_weight, L3_gnn_w_comp, src, dst, edge_type_90), axis=-1)
    return x

_drawn_inputs = setup_inputs


def setup_inputs(seed=0):
    import zlib

    import numpy as np

    out = dict(_drawn_inputs(seed))
    spreads = {'L0_gnn_weight': (1.0, 0.2), 'L1_gnn_b_l': (0.0, 0.1)}
    factors = {}
    for name, (base, spread) in spreads.items():
        noise = np.random.default_rng([zlib.crc32(name.encode()), seed]).standard_normal(out[name].shape)
        drawn = base * np.exp(spread * noise) if base else spread * noise
        out[name] = jnp.asarray(drawn.astype(out[name].dtype))
    for name, factor in factors.items():
        out[name] = (out[name] * factor).astype(out[name].dtype)
    return out
```

```python
import concourse.bass as bass
from concourse import mybir
from contextlib import ExitStack

NODES, EDGES, D = 3125, 103125, 16
P = 128
HI = -(-NODES // P)
GROUPS = 5
BLOCKS = HI // GROUPS
SPAN = BLOCKS * P
PADDED = HI * P
TILES = -(-EDGES // P)
LAST = EDGES - (P - 1) * TILES
T = 13
BATCHES = TILES // T
TURNS = BATCHES // 2
TYPES, RELS, BASES = 8, 90, 30
PARTS = 3
ROW3 = D + 1
CUT = 30
COLS = [PARTS * D + 1, PARTS * D, PARTS * D, PARTS * 2 * D]
STRIDE = [256, 256, 256, 512]
BANKS = [3, 3, 3, 5]
STAGES = 8
EPS = 1e-5


class Steps:

    def __init__(self, sem):
        self.sem, self.base, self.at, self.turn = sem, 0, 0, None

    def mark(self, ins):
        ins.then_inc(self.sem, 1)
        self.at += 1

    def value(self):
        return self.base + self.at + (0 if self.turn is None else self.turn)


def gnn_kernel(nc, a, tables, out):
    fp32, bf16, fp16, i32 = mybir.dt.float32, mybir.dt.bfloat16, mybir.dt.float16, mybir.dt.int32
    ALU, ACT, AX = mybir.AluOpType, mybir.ActivationFunctionType, mybir.AxisListType
    assert BATCHES * T == TILES and TURNS * 2 == BATCHES and BLOCKS * GROUPS == HI

    with ExitStack() as ctx:
        def sb(name, shape, dt=fp32):
            return ctx.enter_context(nc.sbuf_tensor(name, shape, dt))

        def sem(name):
            return ctx.enter_context(nc.semaphore(name))

        edge_i = {n: sb(f"{n}_i", [P, TILES], i32) for n in ("src", "dst", "type8", "type90")}
        rows = [sb(f"row_number{k}", [P, TILES]) for k in range(3)]
        dst_a = sb("dst_a", [P, TILES])
        code = sb("code", [P, TILES])
        in_group = sb("in_group", [P, TILES, GROUPS], bf16)
        edge_w = sb("edge_w", [P, TILES])
        attr = sb("attr", [P, TILES, D])
        attr_score = sb("attr_score", [P, TILES])
        dst_f = attr_score
        row_ring = sb("row_ring", [P, 2, T], i32)
        code_ring = sb("code_ring", [P, 2, T])
        gathered_rows = sb("gathered_rows", [P, 2, T, ROW3])
        onehot = sb("onehot", [P, 2, T, BLOCKS * P], bf16)
        moving = sb("moving", [P, 2, T * GROUPS * COLS[3]], bf16)
        score = sb("score", [P, T])
        attr_tmp = sb("attr_tmp", [P, T, D])
        message = sb("message", [P, T, 2 * D])
        rest = sb("rest", [P, T, 2 * D])
        parts = sb("parts", [P, 2, T * COLS[3]], bf16)
        cat = sb("cat", [P, HI, 2 * D])
        catT = sb("catT", [2 * D, PADDED])
        agg = sb("agg", [P, HI, D])
        agg2 = sb("agg2", [P, HI, D])
        y = sb("y", [P, HI, D])
        square = sb("square", [P, HI, D])
        mean = sb("mean", [P, HI])
        var = sb("var", [P, HI])
        inv_count = sb("inv_count", [P, HI])
        gates = sb("gates", [P, HI, 4 * D])
        table2 = attr[:].rearrange("p t d -> p (t d)")[:, 0:HI * TYPES * D].rearrange("p (h c) -> p h c", h=HI)
        table3 = attr[:].rearrange("p t d -> p (t d)")[:, 0:STAGES * RELS * ROW3].rearrange("p (s c) -> p s c", s=STAGES)
        diff = sb("diff", [P, P])
        ident = sb("ident", [P, P])
        count_i = sb("count_i", [P, BLOCKS * P], i32)
        count = sb("count", [P, BLOCKS * P], fp16)
        zeros = sb("zeros", [P, 512], bf16)
        eps = sb("eps", [P, 1])
        l0_w = sb("l0_w", [P, D])
        l0_self = sb("l0_self", [P, 1])
        l1_w = sb("l1_w", [2 * D, D])
        l1_b = sb("l1_b", [P, D])
        emb = sb("emb", [D, TYPES, D])
        gate_w = sb("gate_w", [2 * D, 4 * D])
        b_ih = sb("b_ih", [P, 3 * D])
        b_hh = sb("b_hh", [P, 3 * D])
        gate_b = sb("gate_b", [P, 4 * D])
        ws = sb("ws", [D, D])
        waT = sb("waT", [D, 3])
        wa_wide = sb("wa_wide", [D, 2, P])
        score_w = sb("score_w", [D, 1])
        score_wide = sb("score_wide", [P, 2, D])
        bases = sb("bases", [BASES, D, D])
        compT = sb("compT", [BASES, RELS])
        wrel_rows = sb("wrel_rows", [RELS, D * D])
        wrel = sb("wrel", [D, RELS, ROW3])
        sums = ctx.enter_context(nc.psum_tensor("sums", [P, 5 * 512], fp32))
        nodes = ctx.enter_context(nc.psum_tensor("nodes", [P, 3, 512], fp32))

        cleared = sem("cleared")
        loaded = {n: sem(f"loaded_{n}") for n in ("dst", "src", "w", "types", "attr", "weights")}
        iota_done = sem("iota_done")
        const_done = sem("const_done")
        x_loaded = sem("x_loaded")
        dve_step = sem("dve_step")
        act_step = sem("act_step")
        edges_ready = [sem(f"edges_ready{k}") for k in range(3)]
        ring_ready = sem("ring_ready")
        gathered = [sem(f"gathered{q}") for q in range(2)]
        taken = sem("taken")
        moving_ready = sem("moving_ready")
        added = sem("added")
        sums_ready = sem("sums_ready")
        sums_taken = sem("sums_taken")
        filled = sem("filled")
        emptied = [sem(f"emptied{b}") for b in range(3)]
        cat_ready = sem("cat_ready")
        catT_ready = sem("catT_ready")
        var_ready = sem("var_ready")
        std_ready = sem("std_ready")
        gate_in = sem("gate_in")
        gate_out = sem("gate_out")
        wide_ready = sem("wide_ready")
        wrel_out = sem("wrel_out")
        wrel_saved = sem("wrel_saved")
        wrel_loaded = sem("wrel_loaded")
        wrel_ready = sem("wrel_ready")
        table_part = sem("table_part")
        table_staged = sem("table_staged")
        pool_turn = sem("pool_turn")
        staged_act, staged_dve = sem("staged_act"), sem("staged_dve")
        table1_saved, table2_saved = sem("table1_saved"), sem("table2_saved")
        table3_saved = [sem(f"table3_saved{s}") for s in range(STAGES)]
        stored = sem("stored")

        def sums_of(layer):
            return sums[:, 0:BLOCKS * STRIDE[layer]].rearrange("p (j c) -> p j c", j=BLOCKS)

        def by_group(t):
            return t.rearrange("p (a j) d -> p j a d", j=BLOCKS)

        def part_of(layer, lo):
            c = COLS[layer]
            return sums_of(layer)[:, :, 0:GROUPS * c].rearrange("p j (a c) -> p j a c", a=GROUPS)[:, :, :, lo:lo + D]

        x = cat[:, :, 0:D]

        XPOSE = -(-HI // 4)
        GATES = -(-HI // 8)
        order = ["wrel", "score_w", "score_wide"]
        order += [f"l1_xpose{g}" for g in range(XPOSE)] + ["l1_linear"]
        order += [f"t2_xpose{g}" for g in range(XPOSE)] + [f"t2_rows{g}" for g in range(XPOSE)]
        order += [f"l2_xpose{g}" for g in range(XPOSE)] + [f"l2_gates{g}" for g in range(GATES)]
        order += [f"t3_xpose{g}" for g in range(XPOSE)] + [f"t3_rows{h}_{c}" for h in range(HI) for c in range(3)]
        fill_no = {n: k for k, n in enumerate(order)}

        def bank(name):
            return nodes[:, fill_no[name] % 3, :]

        def four(g):
            return range(4 * g, min(4 * g + 4, HI))

        block = ctx.enter_context(nc.Block())

        @block.sync
        def _(sp):
            def load_edges(tile, name, s, width=1):
                flat = a[name]
                for lo, hi in ((0, 112), (112, P - 1)):
                    sp.dma_start(tile[lo:hi, :], flat[lo * TILES * width:hi * TILES * width]
                                 .rearrange("(p t) -> p t", p=hi - lo)).then_inc(s, 16)
                sp.dma_start(tile[P - 1:P, 0:LAST * width],
                             flat[(P - 1) * TILES * width:EDGES * width].rearrange("(p t) -> p t", p=1)).then_inc(s, 16)

            sp.wait_ge(cleared, 1)
            load_edges(edge_i["src"], "src", loaded["src"])
            load_edges(edge_i["dst"], "dst", loaded["dst"])
            load_edges(edge_w, "edge_weight", loaded["w"])
            full = NODES // P
            sp.dma_start(cat[:, 0:full, 0:D], a["x"][0:full * P, :].rearrange("(h p) d -> p h d", p=P)).then_inc(x_loaded, 16)
            sp.dma_start(cat[0:NODES - full * P, full, 0:D], a["x"][full * P:NODES, :]).then_inc(x_loaded, 16)
            w = [(l0_w[:], a["L0_gnn_weight"].partition_broadcast(P)),
                 (l0_self[:], a["L0_gnn_self_loop_weight"].partition_broadcast(P)),
                 (l1_w[0:D, :], a["W_rT"]), (l1_w[D:2 * D, :], a["W_lT"]),
                 (l1_b[:], a["L1_gnn_b_l"].partition_broadcast(P)),
                 (emb[:], a["L2_gnn_edge_embT"]),
                 (gate_w[0:D, 0:2 * D], a["w_hhT"][:, 0:2 * D]), (gate_w[0:D, 3 * D:4 * D], a["w_hhT"][:, 2 * D:3 * D]),
                 (gate_w[D:2 * D, 0:3 * D], a["w_ihT"]),
                 (b_ih[:], a["L2_gnn_b_ih"].partition_broadcast(P)), (b_hh[:], a["L2_gnn_b_hh"].partition_broadcast(P)),
                 (ws[:], a["L3_gnn_Ws"]), (waT[:], a["WaT"]), (compT[:], a["w_compT"]), (bases[:], a["bases"])]
            for dst, src in w:
                sp.dma_start(dst, src).then_inc(loaded["weights"], 16)
            load_edges(edge_i["type8"], "edge_type_8", loaded["types"])
            load_edges(edge_i["type90"], "edge_type_90", loaded["types"])
            load_edges(attr[:].rearrange("p t d -> p (t d)"), "edge_attr_16", loaded["attr"], D)

            sp.wait_ge(wrel_out, 1)
            sp.dma_start(tables["wrel"].rearrange("(i r o) -> r i o", i=D, r=RELS),
                         wrel_rows[:].rearrange("r (i o) -> r i o", i=D)).then_inc(wrel_saved, 16)
            sp.wait_ge(wrel_saved, 16)
            sp.dma_start(wrel[:, :, 0:D], tables["wrel"].rearrange("(r i o) -> i r o", r=RELS, i=D)).then_inc(wrel_loaded, 16)

            sp.wait_ge(cat_ready, 1)
            sp.dma_start(tables["rows1"].rearrange("(h p) d -> p h d", p=P), x).then_inc(table1_saved, 16)
            sp.wait_ge(table_staged, 1)
            sp.dma_start(tables["rows2"].rearrange("(h p t) d -> p h (t d)", p=P, t=TYPES), table2).then_inc(table2_saved, 16)
            rows3 = tables["rows3"].rearrange("(h p r) d -> h p (r d)", p=P, r=RELS)
            for h in range(HI):
                sp.wait_ge(staged_act, h + 1 + (h + 2) // 2)
                sp.wait_ge(staged_dve, h + 1 + (h + 1) // 2)
                sp.dma_start(rows3[h], table3[:, h % STAGES, :]).then_inc(table3_saved[h % STAGES], 16)
            sp.wait_ge(cat_ready, 6)
            sp.dma_start(out[0:full * P, :].rearrange("(h p) d -> p h d", p=P), cat[:, 0:full, 0:D]).then_inc(stored, 16)
            sp.dma_start(out[full * P:NODES, :], cat[0:NODES - full * P, full, 0:D]).then_inc(stored, 16)
            sp.wait_ge(stored, 32)

        @block.gpsimd
        def _(pool):
            nc.gpsimd.iota(count_i[:], pattern=[[1, BLOCKS * P]], base=0, channel_multiplier=0).then_inc(iota_done, 1)
            nc.gpsimd.iota(diff[:], pattern=[[1, P]], base=0, channel_multiplier=-1,
                           allow_small_or_imprecise_dtypes=True).then_inc(iota_done, 1)
            for layer in range(4):
                table = (a["x"], tables["rows1"], tables["rows2"], tables["rows3"])[layer]
                width = ROW3 if layer == 3 else D
                if layer == 1:
                    pool.wait_ge(table1_saved, 16)
                if layer == 2:
                    pool.wait_ge(table2_saved, 16)
                if layer == 3:
                    for s in range(STAGES):
                        pool.wait_ge(table3_saved[s], 16 * len(range(s, HI, STAGES)))
                with pool.Fori(0, TURNS) as i:
                    for q in range(2):
                        pool.wait_ge(ring_ready, i * 2 + (layer * BATCHES + q + 1))
                        pool.sem_inc(pool_turn, 1)
                        for t in range(T):
                            nc.gpsimd.indirect_dma_start(
                                gathered_rows[:, q, t, 0:width], None, table,
                                bass.IndirectOffsetOnAxis(row_ring[:, q, t:t + 1], 0)).then_inc(gathered[q], 16)

        @block.scalar
        def _(act):
            def evacuate(name, dst, src, done, value):
                act.wait_ge(filled, fill_no[name] + 1)
                nc.scalar.copy(dst, src).then_inc(done, 1)
                act.wait_ge(done, value)
                act.sem_inc(emptied[fill_no[name] % 3], 1)

            def transpose_out(step, rows, base):
                for g in range(XPOSE):
                    n = 128 * len(four(g))
                    evacuate(f"{step}_xpose{g}", catT[0:rows, 512 * g:512 * g + n],
                             bank(f"{step}_xpose{g}")[0:rows, 0:n], catT_ready, base + g + 1)

            def feed(layer):
                numbers = rows[max(0, layer - 1)]
                with act.Fori(0, TURNS) as i:
                    for q in range(2):
                        act.wait_ge(taken, i * 2 + (layer * BATCHES + q + 1))
                        nc.scalar.copy(row_ring[:, q, :], numbers[:, bass.ds(i * (2 * T) + q * T, T)]).then_inc(act_step, 1)
                        nc.scalar.copy(code_ring[:, q, :], code[:, bass.ds(i * (2 * T) + q * T, T)]).then_inc(act_step, 1)
                        act.wait_ge(act_step, i * 4 + (layer * 2 * BATCHES + 2 * q + 2))
                        act.sem_inc(ring_ready, 1)

            def root(k):
                act.wait_ge(var_ready, k)
                nc.scalar.activation(var[:], var[:], ACT.Sqrt, bias=eps[:], scale=1.0 / D).then_inc(std_ready, 1)

            evacuate("wrel", wrel_rows[:], bank("wrel")[0:RELS, 0:D * D], wrel_out, 1)
            act.wait_ge(edges_ready[0], 1)
            feed(0)
            root(1)
            act.wait_ge(edges_ready[1], 1)
            feed(1)
            transpose_out("l1", 2 * D, 0)
            root(2)
            transpose_out("t2", D, XPOSE)
            for g in range(XPOSE):
                n = len(four(g))
                evacuate(f"t2_rows{g}", table2[:, 4 * g:4 * g + n, :].rearrange("p h c -> p (h c)"),
                         bank(f"t2_rows{g}")[:, 0:n * P], table_part, g + 1)
            act.sem_inc(table_staged, 1)
            feed(2)
            transpose_out("l2", 2 * D, 2 * XPOSE)
            act.wait_ge(gate_in, 1)
            nc.scalar.activation(gates[:, :, 0:2 * D], gates[:, :, 0:2 * D], ACT.Tanh, scale=0.5).then_inc(gate_out, 1)
            act.wait_ge(gate_in, 2)
            nc.scalar.activation(gates[:, :, 2 * D:3 * D], gates[:, :, 2 * D:3 * D], ACT.Tanh).then_inc(gate_out, 1)
            root(3)
            transpose_out("t3", D, 3 * XPOSE)
            n = 0
            for h in range(HI):
                if h >= STAGES:
                    act.wait_ge(table3_saved[h % STAGES], 16 * (h // STAGES))
                for c in (0, 2) if h % 2 == 0 else (0,):
                    n += 1
                    evacuate(f"t3_rows{h}_{c}", table3[:, h % STAGES, c * CUT * ROW3:(c + 1) * CUT * ROW3],
                             bank(f"t3_rows{h}_{c}")[:, 0:CUT * ROW3], staged_act, n)
            feed(3)
            root(4)

        @block.vector
        def _(dve):
            step = Steps(dve_step)

            def link(ins):
                step.mark(ins)
                dve.wait_ge(step.sem, step.value())

            V = nc.vector
            for n in ("src", "type8", "type90"):
                V.memset(edge_i[n][:], 0)
            V.memset(edge_i["dst"][:], -1)
            V.memset(edge_w[:], 0.0)
            V.memset(cat[:], 0.0)
            V.memset(gate_w[:], 0.0)
            link(V.memset(attr[96:P, :, :], 0.0))
            dve.sem_inc(cleared, 1)
            V.memset(zeros[:], 0.0)
            V.memset(eps[:], EPS)
            dve.wait_ge(iota_done, 2)
            V.tensor_copy(count[:], count_i[:])
            link(V.tensor_scalar(ident[:], diff[:], 0.0, None, ALU.is_equal))
            dve.sem_inc(const_done, 1)

            dve.wait_ge(loaded["dst"], 48)
            link(V.tensor_copy(dst_f[:], edge_i["dst"][:]))
            link(V.tensor_scalar(dst_a[:], dst_f[:], float(SPAN), None, ALU.is_ge))
            for k in range(2, GROUPS):
                link(V.scalar_tensor_tensor(dst_a[:], dst_f[:], float(SPAN * k), dst_a[:], ALU.is_ge, ALU.add))
            V.scalar_tensor_tensor(code[:], dst_a[:], -float(SPAN), dst_f[:], ALU.mult, ALU.add)
            for k in range(GROUPS):
                V.tensor_scalar(in_group[:, :, k], dst_a[:], float(k), None, ALU.is_equal)
            dve.wait_ge(loaded["src"], 48)
            link(V.tensor_copy(rows[0][:], edge_i["src"][:]))
            dve.sem_inc(edges_ready[0], 1)
            dve.wait_ge(loaded["types"], 96)
            V.scalar_tensor_tensor(rows[1][:], rows[0][:], float(TYPES), edge_i["type8"][:], ALU.mult, ALU.add)
            link(V.scalar_tensor_tensor(rows[2][:], rows[0][:], float(RELS), edge_i["type90"][:], ALU.mult, ALU.add))
            dve.sem_inc(edges_ready[1], 1)
            dve.wait_ge(loaded["weights"], 16 * 15)
            link(V.tensor_copy(wa_wide[:], waT[:, 1:3].unsqueeze(2).to_broadcast([D, 2, P])))
            dve.sem_inc(wide_ready, 1)
            V.tensor_tensor(gate_b[:, 0:2 * D], b_ih[:, 0:2 * D], b_hh[:, 0:2 * D], ALU.add)
            V.tensor_copy(gate_b[:, 2 * D:3 * D], b_ih[:, 2 * D:3 * D])
            link(V.tensor_copy(gate_b[:, 3 * D:4 * D], b_hh[:, 2 * D:3 * D]))

            def empty(name, ins_of):
                dve.wait_ge(filled, fill_no[name] + 1)
                link(ins_of(bank(name)))
                dve.sem_inc(emptied[fill_no[name] % 3], 1)

            empty("score_w", lambda b: V.tensor_copy(score_w[:], b[0:D, 0:1]))
            empty("score_wide", lambda b: V.tensor_copy(score_wide[:].rearrange("p k d -> p (k d)"), b[:, 0:2 * D]))
            dve.wait_ge(loaded["attr"], 48)
            dve.wait_ge(loaded["w"], 48)
            dve.sem_inc(taken, 2)

            def scatter(layer):
                c = COLS[layer]
                d = 2 * D if layer == 3 else D
                marks = {0: 8, 1: 4, 2: 4, 3: 7}[layer]
                step.base, step.at = step.base + step.at, 0
                with dve.Fori(0, TURNS) as i:
                    step.turn = i * (2 * marks)
                    for q in range(2):
                        now = i * 2 + (layer * BATCHES + q + 1)
                        tiles = bass.ds(i * (2 * T) + q * T, T)
                        mov = moving[:, q, 0:T * GROUPS * c].rearrange("p (t a c) -> p t a c", t=T, a=GROUPS)
                        par = parts[:, q, 0:T * c].rearrange("p (t c) -> p t c", t=T)
                        got = gathered_rows[:, q, :, 0:D]
                        dve.wait_ge(ring_ready, now)
                        dve.wait_ge(added, now)
                        for t in range(T):
                            V.tensor_scalar(onehot[:, q, t, :], count[:], code_ring[:, q, t:t + 1], None, ALU.is_equal)
                        if layer == 0:
                            link(V.tensor_tensor(attr_tmp[:], attr[:, tiles, :],
                                                 score_wide[:, 0, :].unsqueeze(1).to_broadcast([P, T, D]), ALU.mult))
                            step.mark(V.tensor_reduce(attr_score[:, tiles], attr_tmp[:], AX.X, ALU.add))
                            step.mark(V.memset(par[:, :, c - 1], 1.0))
                        dve.wait_ge(gathered[q], i * (16 * T) + (layer * TURNS + 1) * 16 * T)
                        msg = got
                        if layer == 0:
                            msg = message[:, :, 0:D]
                            link(V.tensor_tensor(msg, got, edge_w[:, tiles].unsqueeze(2).to_broadcast([P, T, D]), ALU.mult))
                        if layer == 3:
                            msg = message[:]
                            step.mark(V.tensor_copy(message[:, :, 0:D], got))
                            link(V.tensor_tensor(score[:], gathered_rows[:, q, :, D], attr_score[:, tiles], ALU.add))
                            link(V.tensor_tensor(message[:, :, D:2 * D], got, score[:].unsqueeze(2).to_broadcast([P, T, D]), ALU.mult))
                        link(V.tensor_copy(par[:, :, 0:d], msg))
                        link(V.tensor_tensor(rest[:, :, 0:d], msg, par[:, :, 0:d], ALU.subtract))
                        link(V.tensor_copy(par[:, :, d:2 * d], rest[:, :, 0:d]))
                        link(V.tensor_tensor(par[:, :, 2 * d:3 * d], rest[:, :, 0:d], par[:, :, d:2 * d], ALU.subtract))
                        dve.sem_inc(taken, 1)
                        V.tensor_tensor(mov, par.unsqueeze(2).to_broadcast([P, T, GROUPS, c]),
                                        in_group[:, tiles, :].unsqueeze(3).to_broadcast([P, T, GROUPS, c]),
                                        ALU.mult).then_inc(moving_ready, 1)
                assert step.at == 2 * marks, (layer, step.at)
                step.base, step.at, step.turn = step.base + TURNS * 2 * marks, 0, None
                dve.wait_ge(sums_ready, layer + 1)

            def sum_parts(dst, layer, lo, d):
                link(V.tensor_copy(by_group(dst), part_of(layer, lo)))
                for k in range(1, PARTS):
                    link(V.tensor_tensor(by_group(dst), by_group(dst), part_of(layer, lo + k * d), ALU.add))

            def wide(t, n=D):
                return t.unsqueeze(1).to_broadcast([P, HI, n])

            def each(t):
                return t.unsqueeze(2).to_broadcast([P, HI, D])

            def norm(layer, ready):
                link(V.tensor_reduce(mean[:], y[:], AX.X, ALU.add))
                link(V.tensor_scalar(mean[:], mean[:], 1.0 / D, None, ALU.mult))
                link(V.tensor_tensor(y[:], y[:], each(mean[:]), ALU.subtract))
                link(V.tensor_tensor(square[:], y[:], y[:], ALU.mult))
                V.tensor_reduce(var[:], square[:], AX.X, ALU.add).then_inc(var_ready, 1)
                dve.wait_ge(std_ready, layer + 1)
                link(V.reciprocal(mean[:], var[:]))
                link(V.tensor_tensor(x, y[:], each(mean[:]), ALU.mult))
                dve.sem_inc(cat_ready, 1)

            scatter(0)
            sum_parts(agg, 0, 0, D)
            counts = sums_of(0)[:, :, 0:GROUPS * COLS[0]].rearrange("p j (a c) -> p j a c", a=GROUPS)[:, :, :, COLS[0] - 1]
            link(V.tensor_scalar(inv_count[:].rearrange("p (a j) -> p j a", j=BLOCKS), counts, 1.0, None, ALU.max))
            dve.sem_inc(sums_taken, 1)
            link(V.reciprocal(inv_count[:], inv_count[:]))
            dve.wait_ge(x_loaded, 32)
            link(V.tensor_tensor(agg[:], agg[:], wide(l0_w[:]), ALU.mult))
            link(V.scalar_tensor_tensor(agg[:], x, l0_self[:], agg[:], ALU.mult, ALU.add))
            link(V.tensor_tensor(agg[:], agg[:], x, ALU.add))
            link(V.tensor_scalar(agg[:], agg[:], 0.0, 1.0, ALU.max, ALU.min))
            link(V.tensor_tensor(y[:], agg[:], x, ALU.add))
            norm(0, 1)

            scatter(1)
            sum_parts(agg, 1, 0, D)
            dve.sem_inc(sums_taken, 1)
            link(V.tensor_tensor(cat[:, :, D:2 * D], agg[:], each(inv_count[:]), ALU.mult))
            dve.sem_inc(cat_ready, 1)
            link(V.tensor_tensor(agg[:], x, wide(l1_b[:]), ALU.add))
            empty("l1_linear", lambda b: V.tensor_tensor(y[:].rearrange("p h d -> p (h d)"), b[:, 0:HI * D],
                                                         agg[:].rearrange("p h d -> p (h d)"), ALU.add))
            norm(1, 3)

            scatter(2)
            sum_parts(agg, 2, 0, D)
            dve.sem_inc(sums_taken, 1)
            link(V.tensor_copy(cat[:, :, D:2 * D], agg[:]))
            dve.sem_inc(cat_ready, 1)
            for g in range(GATES):
                n = min(8, HI - 8 * g)
                empty(f"l2_gates{g}", lambda b: V.tensor_tensor(
                    gates[:, 8 * g:8 * g + n, :], b[:, 0:n * 4 * D].rearrange("p (h c) -> p h c", h=n),
                    gate_b[:].unsqueeze(1).to_broadcast([P, n, 4 * D]), ALU.add))
            dve.sem_inc(gate_in, 1)
            dve.wait_ge(gate_out, 1)
            link(V.tensor_scalar(gates[:, :, 0:2 * D], gates[:, :, 0:2 * D], 0.5, 0.5, ALU.mult, ALU.add))
            link(V.tensor_tensor(agg[:], gates[:, :, 0:D], gates[:, :, 3 * D:4 * D], ALU.mult))
            V.tensor_tensor(gates[:, :, 2 * D:3 * D], gates[:, :, 2 * D:3 * D], agg[:], ALU.add).then_inc(gate_in, 1)
            dve.wait_ge(gate_out, 2)
            new = gates[:, :, 2 * D:3 * D]
            link(V.tensor_tensor(agg[:], x, new, ALU.subtract))
            link(V.tensor_tensor(agg[:], agg[:], gates[:, :, D:2 * D], ALU.mult))
            link(V.tensor_tensor(agg[:], agg[:], new, ALU.add))
            link(V.tensor_tensor(y[:], agg[:], x, ALU.add))
            dve.wait_ge(wrel_loaded, 16)
            link(V.tensor_copy(wrel[:, :, D:ROW3], score_w[:].unsqueeze(1).to_broadcast([D, RELS, 1])))
            dve.sem_inc(wrel_ready, 1)
            norm(2, 5)
            n = 0
            for h in range(HI):
                if h >= STAGES:
                    dve.wait_ge(table3_saved[h % STAGES], 16 * (h // STAGES))
                for c in (1,) if h % 2 == 0 else (1, 2):
                    name = f"t3_rows{h}_{c}"
                    dve.wait_ge(filled, fill_no[name] + 1)
                    n += 1
                    V.tensor_copy(table3[:, h % STAGES, c * CUT * ROW3:(c + 1) * CUT * ROW3],
                                  bank(name)[:, 0:CUT * ROW3]).then_inc(staged_dve, 1)
                    dve.wait_ge(staged_dve, n)
                    dve.sem_inc(emptied[fill_no[name] % 3], 1)

            scatter(3)
            sum_parts(agg, 3, 0, 2 * D)
            sum_parts(agg2, 3, D, 2 * D)
            link(V.tensor_tensor(square[:], x, wide(score_wide[:, 1, :]), ALU.mult))
            link(V.tensor_reduce(mean[:], square[:], AX.X, ALU.add))
            link(V.tensor_tensor(agg[:], agg[:], each(mean[:]), ALU.mult))
            link(V.tensor_tensor(agg[:], agg[:], agg2[:], ALU.add))
            link(V.tensor_tensor(y[:], agg[:], x, ALU.add))
            norm(3, 6)

        @block.tensor
        def _(pe):
            def start(name):
                n = fill_no[name]
                if n >= 3:
                    pe.wait_ge(emptied[n % 3], n // 3)
                return bank(name)

            def transpose(step, rows):
                for g in range(XPOSE):
                    b = start(f"{step}_xpose{g}")
                    for k, h in enumerate(four(g)):
                        last = nc.tensor.transpose(b[0:rows, k * P:(k + 1) * P], cat[:, h, 0:rows], ident[:])
                    last.then_inc(filled, 1)

            def scatter(layer):
                c = COLS[layer]
                pe.wait_ge(sums_taken, layer) if layer else None
                for b in range(BANKS[layer]):
                    nc.tensor.matmul(sums[:, 512 * b:512 * b + 512], zeros[:, 0:P], zeros[:], start=True, stop=False)
                with pe.Fori(0, TURNS) as i:
                    for q in range(2):
                        pe.wait_ge(moving_ready, i * 2 + (layer * BATCHES + q + 1))
                        mov = moving[:, q, 0:T * GROUPS * c].rearrange("p (t c) -> p t c", t=T)
                        for t in range(T):
                            for j in range(BLOCKS):
                                last = nc.tensor.matmul(sums_of(layer)[:, j, 0:GROUPS * c], onehot[:, q, t, j * P:(j + 1) * P],
                                                        mov[:, t, :], start=False, stop=False, skip_group_check=True)
                        last.then_inc(added, 1)
                for b in range(BANKS[layer]):
                    last = nc.tensor.matmul(sums[:, 512 * b:512 * b + 512], zeros[:, 0:P], zeros[:], start=False, stop=True)
                last.then_inc(sums_ready, 1)

            pe.wait_ge(const_done, 1)
            pe.sem_inc(added, 2)
            pe.wait_ge(loaded["weights"], 16 * 15)
            nc.tensor.matmul(start("wrel")[0:RELS, 0:D * D], compT[:], bases[:].rearrange("b i o -> b (i o)"),
                             start=True, stop=True).then_inc(filled, 1)
            nc.tensor.matmul(start("score_w")[0:D, 0:1], ws[:], waT[:, 0:1], start=True, stop=True).then_inc(filled, 1)
            b = start("score_wide")
            pe.wait_ge(wide_ready, 1)
            for k in range(2):
                last = nc.tensor.matmul(b[:, k * D:(k + 1) * D], wa_wide[:, k, :], ws[:], start=True, stop=True)
            last.then_inc(filled, 1)

            scatter(0)
            scatter(1)
            pe.wait_ge(cat_ready, 2)
            transpose("l1", 2 * D)
            b = start("l1_linear")
            pe.wait_ge(catT_ready, XPOSE)
            for h in range(HI):
                last = nc.tensor.matmul(b[:, h * D:(h + 1) * D], catT[:, h * P:(h + 1) * P], l1_w[:], start=True, stop=True)
            last.then_inc(filled, 1)
            pe.wait_ge(cat_ready, 3)
            transpose("t2", D)
            pe.wait_ge(catT_ready, 2 * XPOSE)
            for g in range(XPOSE):
                b = start(f"t2_rows{g}")
                for k, h in enumerate(four(g)):
                    last = nc.tensor.matmul(b[:, k * P:(k + 1) * P], catT[0:D, h * P:(h + 1) * P],
                                            emb[:].rearrange("i t o -> i (t o)"), start=True, stop=True)
                last.then_inc(filled, 1)
            scatter(2)
            pe.wait_ge(cat_ready, 4)
            transpose("l2", 2 * D)
            pe.wait_ge(catT_ready, 3 * XPOSE)
            for g in range(GATES):
                b = start(f"l2_gates{g}")
                for k, h in enumerate(range(8 * g, min(8 * g + 8, HI))):
                    last = nc.tensor.matmul(b[:, k * 4 * D:(k + 1) * 4 * D], catT[:, h * P:(h + 1) * P], gate_w[:],
                                            start=True, stop=True)
                last.then_inc(filled, 1)
            pe.wait_ge(cat_ready, 5)
            transpose("t3", D)
            pe.wait_ge(catT_ready, 4 * XPOSE)
            pe.wait_ge(wrel_ready, 1)
            for h in range(HI):
                for c in range(3):
                    b = start(f"t3_rows{h}_{c}")
                    nc.tensor.matmul(b[:, 0:CUT * ROW3], catT[0:D, h * P:(h + 1) * P],
                                     wrel[:, c * CUT:(c + 1) * CUT, :].rearrange("i r o -> i (r o)"),
                                     start=True, stop=True).then_inc(filled, 1)
            scatter(3)


def kernel(**inputs):
    import numpy as _np
    import concourse.bacc as _bacc
    from concourse import mybir as _mybir
    from concourse.bass_utils import run_bass_kernel_spmd as _run

    nc = _bacc.Bacc("TRN2", target_bir_lowering=False, num_devices=1)
    arrays, given = {}, {}

    def give(name, x):
        x = _np.ascontiguousarray(x)
        arrays[f"in_{name}"] = x
        given[name] = nc.dram_tensor(f"in_{name}", x.shape, _mybir.dt.from_np(x.dtype), kind="ExternalInput").ap()

    for name in ("x", "src", "dst", "edge_type_8", "edge_type_90", "edge_weight", "L0_gnn_weight",
                 "L1_gnn_b_l", "L2_gnn_b_ih", "L2_gnn_b_hh", "L3_gnn_Ws"):
        give(name, inputs[name])
    give("edge_attr_16", _np.reshape(inputs["edge_attr_16"], (-1,)))
    give("L0_gnn_self_loop_weight", _np.reshape(inputs["L0_gnn_self_loop_weight"], (1,)))
    give("W_lT", _np.transpose(inputs["L1_gnn_W_l"]))
    give("W_rT", _np.transpose(inputs["L1_gnn_W_r"]))
    give("w_ihT", _np.transpose(inputs["L2_gnn_w_ih"]))
    give("w_hhT", _np.transpose(inputs["L2_gnn_w_hh"]))
    give("L2_gnn_edge_embT", _np.transpose(_np.reshape(inputs["L2_gnn_edge_emb"], (TYPES, D, D)), (2, 0, 1)))
    give("WaT", _np.transpose(_np.reshape(inputs["L3_gnn_Wa"], (3, D))))
    give("w_compT", _np.transpose(inputs["L3_gnn_w_comp"]))
    give("bases", _np.transpose(_np.reshape(inputs["L3_gnn_weight"], (D, BASES, D)), (1, 0, 2)))
    f32 = _mybir.dt.float32
    tables = {
        "wrel": nc.dram_tensor("wrel_flat", (RELS * D * D,), f32).ap(),
        "rows1": nc.dram_tensor("rows1", (PADDED, D), f32).ap(),
        "rows2": nc.dram_tensor("rows2", (PADDED * TYPES, D), f32).ap(),
        "rows3": nc.dram_tensor("rows3", (PADDED * RELS, ROW3), f32).ap(),
    }
    out = nc.dram_tensor("out_0", (NODES, D), f32, kind="ExternalOutput").ap()
    gnn_kernel(nc, given, tables, out)
    r = _run(nc, [arrays], core_ids=[0])
    return r.results[0]["out_0"]
```

```python
import concourse.bass as bass
from concourse import mybir
from contextlib import ExitStack

NODES, EDGES, D = 3125, 103125, 16
P = 128
HI = -(-NODES // P)
GROUPS = 5
BLOCKS = HI // GROUPS
SPAN = BLOCKS * P
PADDED = HI * P
TILES = -(-EDGES // P)
T = 13
FULL = EDGES // (P * T) * T
TAIL = EDGES - FULL * P
BATCHES = TILES // T
TURNS = BATCHES // 2
TYPES, RELS, BASES = 8, 90, 30
PARTS = 3
ROW3 = D + 1
CUT = 30
COLS = [PARTS * D + 1, PARTS * D, PARTS * D, PARTS * 2 * D]
STRIDE = [256, 256, 256, 512]
BANKS = [3, 3, 3, 5]
STAGES = 8
EPS = 1e-5
BY_DMA = [5, 5, 9, 9]
PICKS = [T - n for n in BY_DMA]
PICKED = max(PICKS)
TYPED = PICKS[2]
HALF = 4
CODES = [1, 1, 2, 2]
GD = GROUPS * D
STEP2 = -(-NODES * 2 * P * T // EDGES)
STEP1 = STEP2 // 2
MARGIN = (P - STEP1) // 2
SPREAD = MARGIN + PADDED + 1


class Steps:

    def __init__(self, sem):
        self.sem, self.base, self.at, self.turn = sem, 0, 0, None

    def mark(self, ins):
        ins.then_inc(self.sem, 1)
        self.at += 1

    def value(self):
        return self.base + self.at + (0 if self.turn is None else self.turn)


def gnn_kernel(nc, a, tables, out):
    fp32, bf16, fp16, i32 = mybir.dt.float32, mybir.dt.bfloat16, mybir.dt.float16, mybir.dt.int32
    ALU, ACT, AX = mybir.AluOpType, mybir.ActivationFunctionType, mybir.AxisListType
    assert BATCHES * T == TILES and TURNS * 2 == BATCHES and BLOCKS * GROUPS == HI

    with ExitStack() as ctx:
        def sb(name, shape, dt=fp32):
            return ctx.enter_context(nc.sbuf_tensor(name, shape, dt))

        def sem(name):
            return ctx.enter_context(nc.semaphore(name))

        rows = [sb(f"row_number{k}", [P, TILES]) for k in range(3)]
        code = sb("code", [P, TILES])
        in_group = sb("in_group", [P, TILES, GROUPS], bf16)
        edge_w = sb("edge_w", [P, TILES])
        attr = sb("attr", [P, TILES, D])
        attr_score = sb("attr_score", [P, TILES])
        row_ring = sb("row_ring", [P, 2, T], i32)
        code_ring = sb("code_ring", [P, 2, T])
        gathered_rows = sb("gathered_rows", [P, 2, T, ROW3])
        onehot = sb("onehot", [P, 2, T, BLOCKS * P], bf16)
        moving = sb("moving", [P, 2, T * GROUPS * COLS[3]], bf16)
        score = sb("score", [P, T])
        attr_tmp = sb("attr_tmp", [P, T, D])
        message = sb("message", [P, T, 2 * D])
        rest = sb("rest", [P, T, 2 * D])
        room = onehot[:].rearrange("p q t c -> p (q t c)")
        names = ("src", "dst", "type8", "type90", "start", "dst_f", "dst_a", "src_a", "src_code", "window")
        first = {n: room[:, 2 * k * TILES:2 * (k + 1) * TILES].bitcast(i32 if k < 5 else fp32) for k, n in enumerate(names)}
        edge_i, starts = first, first["start"]
        dst_f, dst_a, src_a, src_code, window = (first[n] for n in names[5:])
        lookup = room[:, 0:2 * GROUPS * PICKED * P].rearrange("p (q j e) -> p q j e", q=2, j=GROUPS)
        near_onehot = room[:, 2 * GROUPS * PICKED * P:(2 * GROUPS * PICKED + 2 * T) * P].rearrange("p (q t c) -> p q t c", q=2, t=T)
        code_all = moving[:, :, 0:PICKED * P].bitcast(fp16)
        masked = moving[:, 0, PICKED * P:PICKED * P + 2 * PICKED * GD].bitcast(fp32)
        at = PICKED * P + 2 * PICKED * GD
        product = moving[:, 0, at:at + 2 * TYPED * D * D].bitcast(fp32)
        type_all = moving[:, 1, PICKED * P:(PICKED + 2 * TYPED) * P].bitcast(fp16).rearrange("p (q e) -> p q e", q=2)
        at = (PICKED + 2 * TYPED) * P
        type_lookup = moving[:, 1, at:at + 2 * TYPED * P].rearrange("p (q e) -> p q e", q=2)
        gates = moving[:, 0, 0:2 * HI * 4 * D].bitcast(fp32).rearrange("p (h c) -> p h c", h=HI)
        type_f = [moving[:].rearrange("p q c -> p (q c)")[:, 2 * k * TILES:2 * (k + 1) * TILES].bitcast(fp32) for k in range(2)]
        source_x = sb("source_x", [P, TYPED, D])
        source_tmp = sb("source_tmp", [P, TYPED, D])
        type_raw = [sb("emb_rows", [TYPES, D * D]), sb("wrel_by_rel", [RELS, D * D])]
        type_rest = sb("type_rest", [RELS, D * D])
        type_parts = [sb("emb_parts", [TYPES, PARTS, D * D], bf16), sb("wrel_parts", [RELS, PARTS, D * D], bf16)]
        spread = sb("spread", [P, SPREAD])
        xparts = sb("xparts", [P, BLOCKS, PARTS, GD], bf16)
        fold = sb("fold", [2 * PARTS * D, 2 * D])
        fold1 = sb("fold1", [COLS[0], D + 1])
        block_code = sb("block_code", [P, GROUPS])
        bounds = sb("bounds", [P, 2])
        ones = sb("ones", [P, 1])
        far = sb("far", [1, 1], i32)
        parts = sb("parts", [P, 2, T * COLS[3]], bf16)
        cat = sb("cat", [P, HI, 2 * D])
        catT = sb("catT", [P, PADDED])
        blocks = -(-TILES // P)
        codesT = catT[:, 0:3 * blocks * P // 2].bitcast(fp16).rearrange("t (k c p) -> t k c p", k=3, c=blocks)
        agg = sb("agg", [P, HI, D])
        agg2 = sb("agg2", [P, HI, D])
        y = sb("y", [P, HI, D])
        square = sb("square", [P, HI, D])
        mean = sb("mean", [P, HI])
        var = sb("var", [P, HI])
        inv_count = sb("inv_count", [P, HI])
        table2 = spread[:, 0:HI * TYPES * D].rearrange("p (h c) -> p h c", h=HI)
        table3 = attr[:].rearrange("p t d -> p (t d)")[:, 0:STAGES * RELS * ROW3].rearrange("p (s c) -> p s c", s=STAGES)
        diff = sb("diff", [P, P])
        ident = sb("ident", [P, P])
        count_i = sb("count_i", [P, BLOCKS * P], i32)
        count = sb("count", [P, BLOCKS * P], fp16)
        zeros = sb("zeros", [P, 512], bf16)
        eps = sb("eps", [P, 1])
        l0_w = sb("l0_w", [P, D])
        l0_self = sb("l0_self", [P, 1])
        l1_w = sb("l1_w", [2 * D, D])
        l1_b = sb("l1_b", [P, D])
        emb = sb("emb", [D, TYPES, D])
        gate_w = sb("gate_w", [2 * D, 4 * D])
        b_ih = sb("b_ih", [P, 3 * D])
        b_hh = sb("b_hh", [P, 3 * D])
        gate_b = sb("gate_b", [P, 4 * D])
        ws = sb("ws", [D, D])
        waT = sb("waT", [D, 3])
        wa_wide = sb("wa_wide", [D, 3, P])
        score_w = sb("score_w", [D, 1])
        score_wide = sb("score_wide", [P, 3, D])
        bases = sb("bases", [BASES, D, D])
        compT = sb("compT", [BASES, RELS])
        wrel_rows = sb("wrel_rows", [RELS, D * D])
        wrel = sb("wrel", [D, RELS, ROW3])
        sums = ctx.enter_context(nc.psum_tensor("sums", [P, 5 * 512], fp32))
        nodes = ctx.enter_context(nc.psum_tensor("nodes", [P, 3, 512], fp32))

        cleared = sem("cleared")
        loaded = {n: sem(f"loaded_{n}") for n in ("dst", "src", "w", "types", "attr", "weights")}
        iota_done = sem("iota_done")
        const_done = sem("const_done")
        x_loaded = sem("x_loaded")
        dve_step = sem("dve_step")
        act_step = sem("act_step")
        edges_ready = [sem(f"edges_ready{k}") for k in range(3)]
        ring_ready = sem("ring_ready")
        gathered = [[sem(f"gathered{k}_{q}") for q in range(2)] for k in range(4)]
        taken = sem("taken")
        moving_ready = sem("moving_ready")
        added = sem("added")
        sums_ready = sem("sums_ready")
        sums_taken = sem("sums_taken")
        filled = sem("filled")
        emptied = [sem(f"emptied{b}") for b in range(3)]
        cat_ready = sem("cat_ready")
        catT_ready = sem("catT_ready")
        var_ready = sem("var_ready")
        std_ready = sem("std_ready")
        gate_in = sem("gate_in")
        gate_out = sem("gate_out")
        wide_ready = sem("wide_ready")
        wrel_out = sem("wrel_out")
        wrel_saved = sem("wrel_saved")
        wrel_loaded = sem("wrel_loaded")
        wrel_ready = sem("wrel_ready")
        table_part = sem("table_part")
        table_staged = sem("table_staged")
        pool_turn = sem("pool_turn")
        staged_act, staged_dve = sem("staged_act"), sem("staged_dve")
        table1_saved, table2_saved = sem("table1_saved"), sem("table2_saved")
        table3_saved = [sem(f"table3_saved{s}") for s in range(STAGES)]
        stored = sem("stored")
        starts_done = sem("starts_done")
        bounds_ready = sem("bounds_ready")
        far_ready = sem("far_ready")
        codesT_part = sem("codesT_part")
        codesT_saved = sem("codesT_saved")
        xparts_ready = sem("xparts_ready")
        code_all_ready = [sem(f"code_all_ready{q}") for q in range(2)]
        types_ready = sem("types_ready")
        type_parts_ready = sem("type_parts_ready")
        by_rel_loaded = sem("by_rel_loaded")
        lookup_ready = sem("lookup_ready")
        picked = sem("picked")
        mask_done = sem("mask_done")
        picked_taken = sem("picked_taken")
        window_taken = sem("window_taken")
        spread_ready = sem("spread_ready")
        near_step = sem("near_step")
        far_step = sem("far_step")

        def sums_of(layer):
            return sums[:, 0:BLOCKS * STRIDE[layer]].rearrange("p (j c) -> p j c", j=BLOCKS)

        def by_group(t):
            return t.rearrange("p (a j) d -> p j a d", j=BLOCKS)

        def part_of(layer, lo):
            c = COLS[layer]
            return sums_of(layer)[:, :, 0:GROUPS * c].rearrange("p j (a c) -> p j a c", a=GROUPS)[:, :, :, lo:lo + D]

        x = cat[:, :, 0:D]

        XPOSE = -(-HI // 4)
        GATES = -(-HI // 8)
        order = ["wrel", "bounds", "codes0_0", "codes0_1", "score_w", "score_wide", "codes1_0", "codes1_1", "codes2_0", "codes2_1"]
        order += [f"l1_xpose{g}" for g in range(XPOSE)] + ["l1_linear"]
        order += [f"t2_xpose{g}" for g in range(XPOSE)] + [f"t2_rows{g}" for g in range(XPOSE)]
        order += [f"l2_xpose{g}" for g in range(XPOSE)] + [f"l2_gates{g}" for g in range(GATES)]
        order += [f"t3_xpose{g}" for g in range(XPOSE)] + [f"t3_rows{h}_{c}" for h in range(HI) for c in range(3)]
        fill_no = {n: k for k, n in enumerate(order)}

        def picked_at(layer, q, t):
            banks = PICKS[layer] // HALF
            return 512 * (banks * q + t // HALF) + GD * (t % HALF)

        def picked_rows(layer, q):
            banks = PICKS[layer] // HALF
            return (sums[:, 512 * banks * q:512 * banks * (q + 1)].rearrange("p (k c) -> p k c", k=banks)[:, :, 0:HALF * GD]
                    .rearrange("p k (r d) -> p k r d", d=D))

        def matrices(q):
            return sums[:, 1024:2048] if q == 0 else nodes[:, 1:3, :].rearrange("p k c -> p (k c)")

        def window_sums(q, c):
            return sums[0:c, 2048:2048 + P] if q == 0 else nodes[0:c, 0, 0:P]

        def folded(h, d):
            at = 512 * (h // T) + d * (h % T) if d == 2 * D else d * h
            return sums[:, at:at + d]

        def bank(name):
            return nodes[:, fill_no[name] % 3, :]

        def four(g):
            return range(4 * g, min(4 * g + 4, HI))

        block = ctx.enter_context(nc.Block())

        @block.sync
        def _(sp):
            def load_edges(tile, name, s, width=1):
                sp.dma_start(tile[:, 0:FULL * width], a[name]).then_inc(s, 16)
                whole = TAIL // T
                sp.dma_start(tile[0:whole, FULL * width:TILES * width],
                             a[name + "_tail"][0:whole * T * width].rearrange("(p t) -> p t", p=whole)).then_inc(s, 16)
                sp.dma_start(tile[whole:whole + 1, FULL * width:(FULL + TAIL - whole * T) * width],
                             a[name + "_tail"][whole * T * width:TAIL * width].rearrange("(p t) -> p t", p=1)).then_inc(s, 16)

            sp.wait_ge(cleared, 1)
            load_edges(edge_i["src"], "src", loaded["src"])
            load_edges(edge_i["dst"], "dst", loaded["dst"])
            load_edges(edge_w, "edge_weight", loaded["w"])
            full = NODES // P
            sp.dma_start(cat[:, 0:full, 0:D], a["x"][0:full * P, :].rearrange("(h p) d -> p h d", p=P)).then_inc(x_loaded, 16)
            sp.dma_start(cat[0:NODES - full * P, full, 0:D], a["x"][full * P:NODES, :]).then_inc(x_loaded, 16)
            w = [(l0_w[:], a["L0_gnn_weight"].partition_broadcast(P)),
                 (l0_self[:], a["L0_gnn_self_loop_weight"].partition_broadcast(P)),
                 (l1_w[0:D, :], a["W_rT"]), (l1_w[D:2 * D, :], a["W_lT"]),
                 (l1_b[:], a["L1_gnn_b_l"].partition_broadcast(P)),
                 (emb[:], a["L2_gnn_edge_embT"]),
                 (gate_w[0:D, 0:2 * D], a["w_hhT"][:, 0:2 * D]), (gate_w[0:D, 3 * D:4 * D], a["w_hhT"][:, 2 * D:3 * D]),
                 (gate_w[D:2 * D, 0:3 * D], a["w_ihT"]),
                 (b_ih[:], a["L2_gnn_b_ih"].partition_broadcast(P)), (b_hh[:], a["L2_gnn_b_hh"].partition_broadcast(P)),
                 (type_raw[0][:], a["L2_gnn_edge_emb"]),
                 (ws[:], a["L3_gnn_Ws"]), (waT[:], a["WaT"]), (compT[:], a["w_compT"]), (bases[:], a["bases"])]
            for dst, src in w:
                sp.dma_start(dst, src).then_inc(loaded["weights"], 16)
            load_edges(edge_i["type8"], "edge_type_8", loaded["types"])
            load_edges(edge_i["type90"], "edge_type_90", loaded["types"])
            load_edges(attr[:].rearrange("p t d -> p (t d)"), "edge_attr_16", loaded["attr"], D)

            sp.wait_ge(wrel_out, 1)
            sp.dma_start(tables["wrel"].rearrange("(i r o) -> r i o", i=D, r=RELS),
                         wrel_rows[:].rearrange("r (i o) -> r i o", i=D)).then_inc(wrel_saved, 16)
            sp.wait_ge(wrel_saved, 16)
            sp.dma_start(wrel[:, :, 0:D], tables["wrel"].rearrange("(r i o) -> i r o", r=RELS, i=D)).then_inc(wrel_loaded, 16)

            sp.dma_start(type_raw[1][:], tables["wrel"].rearrange("(r c) -> r c", r=RELS)).then_inc(by_rel_loaded, 16)
            whole = TILES // P
            for k in range(3):
                sp.wait_ge(codesT_part, 2 * (k + 1))
                codes = tables["codes"][k * TILES * P:(k + 1) * TILES * P].rearrange("(t p) -> t p", p=P)
                sp.dma_start(codes[0:whole * P, :].rearrange("(c t) p -> t c p", t=P), codesT[:, k, 0:whole, :]).then_inc(codesT_saved, 16)
                sp.dma_start(codes[whole * P:TILES, :], codesT[0:TILES - whole * P, k, whole, :]).then_inc(codesT_saved, 16)
            sp.wait_ge(codesT_saved, 96)
            sp.wait_ge(far_ready, 1)
            is_far = sp.alloc_register("is_far_sp")
            sp.reg_load(is_far, far[0:1, 0:1])

            def send_codes(layer):
                n = PICKS[layer] * P

                def send(b, q):
                    at = b * (T * P) + BY_DMA[layer] * P
                    sp.dma_start(code_all[:, q, 0:n], tables["codes"][bass.ds(at, n)].partition_broadcast(P)).then_inc(code_all_ready[q], 16)
                    if CODES[layer] == 2:
                        at = at + (layer - 1) * TILES * P
                        sp.dma_start(type_all[:, q, 0:n], tables["codes"][bass.ds(at, n)].partition_broadcast(P)).then_inc(code_all_ready[q], 16)

                if layer:
                    sp.wait_ge(lookup_ready, layer * BATCHES)
                send(0, 0)
                send(1, 1)
                with sp.Fori(0, TURNS - 1) as i:
                    for q in range(2):
                        sp.wait_ge(lookup_ready, i * 2 + (layer * BATCHES + q + 1))
                        send(i * 2 + 2 + q, q)

            with sp.If_eq(is_far, 0):
                send_codes(0)
            sp.wait_ge(cat_ready, 1)
            sp.dma_start(tables["rows1"].rearrange("(h p) d -> p h d", p=P), x).then_inc(table1_saved, 16)
            with sp.If_eq(is_far, 0):
                send_codes(1)
            sp.wait_ge(table_staged, 1)
            sp.dma_start(tables["rows2"].rearrange("(h p t) d -> p h (t d)", p=P, t=TYPES), table2).then_inc(table2_saved, 16)
            with sp.If_eq(is_far, 0):
                send_codes(2)
            rows3 = tables["rows3"].rearrange("(h p r) d -> h p (r d)", p=P, r=RELS)
            for h in range(HI):
                sp.wait_ge(staged_act, h + 1 + (h + 2) // 2)
                sp.wait_ge(staged_dve, h + 1 + (h + 1) // 2)
                sp.dma_start(rows3[h], table3[:, h % STAGES, :]).then_inc(table3_saved[h % STAGES], 16)
            with sp.If_eq(is_far, 0):
                send_codes(3)
            sp.wait_ge(cat_ready, 6)
            sp.dma_start(out[0:full * P, :].rearrange("(h p) d -> p h d", p=P), cat[:, 0:full, 0:D]).then_inc(stored, 16)
            sp.dma_start(out[full * P:NODES, :], cat[0:NODES - full * P, full, 0:D]).then_inc(stored, 16)
            sp.wait_ge(stored, 32)

        @block.gpsimd
        def _(pool):
            nc.gpsimd.iota(count_i[:], pattern=[[1, BLOCKS * P]], base=0, channel_multiplier=0).then_inc(iota_done, 1)
            nc.gpsimd.iota(diff[:], pattern=[[1, P]], base=0, channel_multiplier=-1,
                           allow_small_or_imprecise_dtypes=True).then_inc(iota_done, 1)
            nc.gpsimd.iota(starts, pattern=[[STEP2, TURNS], [STEP1, 2], [0, T]], base=-MARGIN,
                           channel_multiplier=0).then_inc(starts_done, 1)
            pool.wait_ge(far_ready, 1)
            is_far = pool.alloc_register("is_far_pool")
            pool.reg_load(is_far, far[0:1, 0:1])

            def gather(layer, tiles):
                table = (a["x"], tables["rows1"], tables["rows2"], tables["rows3"])[layer]
                width = ROW3 if layer == 3 else D
                with pool.Fori(0, TURNS) as i:
                    for q in range(2):
                        pool.wait_ge(ring_ready, i * 2 + (layer * BATCHES + q + 1))
                        pool.sem_inc(pool_turn, 1)
                        for t in range(tiles):
                            nc.gpsimd.indirect_dma_start(
                                gathered_rows[:, q, t, 0:width], None, table,
                                bass.IndirectOffsetOnAxis(row_ring[:, q, t:t + 1], 0)).then_inc(gathered[layer][q], 16)

            for layer in range(4):
                if layer == 1:
                    pool.wait_ge(table1_saved, 16)
                if layer == 2:
                    pool.wait_ge(table2_saved, 16)
                if layer == 3:
                    for s in range(STAGES):
                        pool.wait_ge(table3_saved[s], 16 * len(range(s, HI, STAGES)))
                with pool.If_eq(is_far, 0):
                    gather(layer, BY_DMA[layer])
                with pool.Else():
                    gather(layer, T)

        @block.scalar
        def _(act):
            def evacuate(name, dst, src, done, value):
                act.wait_ge(filled, fill_no[name] + 1)
                nc.scalar.copy(dst, src).then_inc(done, 1)
                act.wait_ge(done, value)
                act.sem_inc(emptied[fill_no[name] % 3], 1)

            def transpose_out(step, rows, base):
                for g in range(XPOSE):
                    n = 128 * len(four(g))
                    evacuate(f"{step}_xpose{g}", catT[0:rows, 512 * g:512 * g + n],
                             bank(f"{step}_xpose{g}")[0:rows, 0:n], catT_ready, base + g + 1)

            def feed(layer):
                numbers = rows[max(0, layer - 1)]
                with act.Fori(0, TURNS) as i:
                    for q in range(2):
                        act.wait_ge(taken, i * 2 + (layer * BATCHES + q + 1))
                        nc.scalar.copy(row_ring[:, q, :], numbers[:, bass.ds(i * (2 * T) + q * T, T)]).then_inc(act_step, 1)
                        nc.scalar.copy(code_ring[:, q, :], code[:, bass.ds(i * (2 * T) + q * T, T)]).then_inc(act_step, 1)
                        act.wait_ge(act_step, i * 4 + (layer * 2 * BATCHES + 2 * q + 2))
                        act.sem_inc(ring_ready, 1)

            def root(k):
                act.wait_ge(var_ready, k)
                nc.scalar.activation(var[:], var[:], ACT.Sqrt, bias=eps[:], scale=1.0 / D).then_inc(std_ready, 1)

            evacuate("wrel", wrel_rows[:], bank("wrel")[0:RELS, 0:D * D], wrel_out, 1)
            def codes_out(k):
                last, n = TILES % P, -(-TILES // P) - 5
                evacuate(f"codes{k}_0", codesT[:, k, 0:4, :].rearrange("t c p -> t (c p)"), bank(f"codes{k}_0"), codesT_part, 2 * k + 1)
                b = bank(f"codes{k}_1")
                act.wait_ge(filled, fill_no[f"codes{k}_1"] + 1)
                nc.scalar.copy(codesT[:, k, 4:4 + n, :].rearrange("t c p -> t (c p)"), b[:, 0:n * P])
                nc.scalar.copy(codesT[0:last, k, 4 + n, :], b[0:last, n * P:(n + 1) * P]).then_inc(codesT_part, 1)
                act.wait_ge(codesT_part, 2 * k + 2)
                act.sem_inc(emptied[fill_no[f"codes{k}_1"] % 3], 1)

            for k in range(3):
                codes_out(k)
            act.wait_ge(edges_ready[0], 1)
            feed(0)
            root(1)
            act.wait_ge(edges_ready[1], 1)
            feed(1)
            transpose_out("l1", 2 * D, 0)
            root(2)
            transpose_out("t2", D, XPOSE)
            for g in range(XPOSE):
                n = len(four(g))
                evacuate(f"t2_rows{g}", table2[:, 4 * g:4 * g + n, :].rearrange("p h c -> p (h c)"),
                         bank(f"t2_rows{g}")[:, 0:n * P], table_part, g + 1)
            act.sem_inc(table_staged, 1)
            feed(2)
            transpose_out("l2", 2 * D, 2 * XPOSE)
            act.wait_ge(gate_in, 1)
            nc.scalar.activation(gates[:, :, 0:2 * D], gates[:, :, 0:2 * D], ACT.Tanh, scale=0.5).then_inc(gate_out, 1)
            act.wait_ge(gate_in, 2)
            nc.scalar.activation(gates[:, :, 2 * D:3 * D], gates[:, :, 2 * D:3 * D], ACT.Tanh).then_inc(gate_out, 1)
            root(3)
            transpose_out("t3", D, 3 * XPOSE)
            n = 0
            for h in range(HI):
                if h >= STAGES:
                    act.wait_ge(table3_saved[h % STAGES], 16 * (h // STAGES))
                for c in (0, 2) if h % 2 == 0 else (0,):
                    n += 1
                    evacuate(f"t3_rows{h}_{c}", table3[:, h % STAGES, c * CUT * ROW3:(c + 1) * CUT * ROW3],
                             bank(f"t3_rows{h}_{c}")[:, 0:CUT * ROW3], staged_act, n)
            feed(3)
            root(4)

        @block.vector
        def _(dve):
            step = Steps(dve_step)

            def link(ins):
                step.mark(ins)
                dve.wait_ge(step.sem, step.value())

            V = nc.vector
            for n in ("src", "type8", "type90"):
                V.memset(edge_i[n][96:P, FULL:TILES], 0)
            V.memset(edge_i["dst"][96:P, FULL:TILES], NODES)
            V.memset(edge_w[96:P, FULL:TILES], 0.0)
            V.memset(attr[96:P, FULL:TILES, :], 0.0)
            V.memset(cat[:], 0.0)
            link(V.memset(gate_w[:], 0.0))
            dve.sem_inc(cleared, 1)
            V.memset(zeros[:], 0.0)
            V.memset(ones[:], 1.0)
            V.memset(spread[:], 0.0)
            V.memset(eps[:], EPS)
            dve.wait_ge(iota_done, 2)
            V.tensor_copy(count[:], count_i[:])
            for j in range(BLOCKS):
                V.tensor_scalar(block_code[:, j:j + 1], diff[:, 0:1], -1.0, float(P * j), ALU.mult, ALU.add)
            link(V.tensor_scalar(ident[:], diff[:], 0.0, None, ALU.is_equal))
            dve.sem_inc(const_done, 1)
            n, m = 2 * PARTS * D, 2 * D
            link(V.tensor_tensor(fold[:], ident[0:n, 0:m], ident[0:n, m:2 * m], ALU.add))
            V.tensor_tensor(fold[:], fold[:], ident[0:n, 2 * m:3 * m], ALU.add)
            link(V.tensor_tensor(fold1[:, 0:D], ident[0:COLS[0], 0:D], ident[0:COLS[0], D:2 * D], ALU.add))
            V.tensor_tensor(fold1[:, 0:D], fold1[:, 0:D], ident[0:COLS[0], 2 * D:3 * D], ALU.add)
            link(V.tensor_copy(fold1[:, D:D + 1], ident[0:COLS[0], COLS[0] - 1:COLS[0]]))

            dve.wait_ge(loaded["dst"], 48)
            link(V.tensor_copy(dst_f, edge_i["dst"]))
            dve.wait_ge(starts_done, 1)
            link(V.tensor_tensor(window, dst_f, starts, ALU.subtract))
            V.tensor_reduce(bounds[:, 0:1], window, AX.X, ALU.max)
            link(V.tensor_reduce(bounds[:, 1:2], window, AX.X, ALU.min))
            link(V.tensor_scalar(bounds[:, 0:1], bounds[:, 0:1], float(P), None, ALU.is_ge))
            link(V.scalar_tensor_tensor(bounds[:, 1:2], bounds[:, 1:2], 0.0, bounds[:, 0:1], ALU.is_lt, ALU.add))
            dve.sem_inc(bounds_ready, 1)

            def split_by_span(f, group, rest):
                link(V.tensor_scalar(group, f, float(SPAN), None, ALU.is_ge))
                for k in range(2, GROUPS):
                    link(V.scalar_tensor_tensor(group, f, float(SPAN * k), group, ALU.is_ge, ALU.add))
                link(V.scalar_tensor_tensor(rest, group, -float(SPAN), f, ALU.mult, ALU.add))

            dve.wait_ge(loaded["src"], 48)
            link(V.tensor_copy(rows[0][:], edge_i["src"]))
            split_by_span(rows[0][:], src_a, src_code)
            dve.sem_inc(edges_ready[2], 1)
            split_by_span(dst_f, dst_a, code[:])

            def empty(name, ins_of):
                dve.wait_ge(filled, fill_no[name] + 1)
                link(ins_of(bank(name)))
                dve.sem_inc(emptied[fill_no[name] % 3], 1)

            empty("bounds", lambda b: V.tensor_copy(far[:], b[0:1, 0:1]))
            dve.sem_inc(far_ready, 1)
            is_far = dve.alloc_register("is_far_dve")
            dve.reg_load(is_far, far[0:1, 0:1])
            near, away = Steps(near_step), Steps(far_step)
            with dve.If_eq(is_far, 0):
                V.tensor_copy(code[:], window)
                for k in range(GROUPS):
                    V.tensor_scalar(in_group[:, :, k], src_a, float(k), None, ALU.is_equal)
            with dve.Else():
                for k in range(GROUPS):
                    V.tensor_scalar(in_group[:, :, k], dst_a, float(k), None, ALU.is_equal)
            link(V.tensor_copy(score[:, 0:1], eps[:]))
            dve.sem_inc(edges_ready[0], 1)
            dve.wait_ge(loaded["types"], 96)
            V.scalar_tensor_tensor(rows[1][:], rows[0][:], float(TYPES), edge_i["type8"], ALU.mult, ALU.add)
            link(V.scalar_tensor_tensor(rows[2][:], rows[0][:], float(RELS), edge_i["type90"], ALU.mult, ALU.add))
            dve.sem_inc(edges_ready[1], 1)
            V.tensor_copy(type_f[0], edge_i["type8"])
            link(V.tensor_copy(type_f[1], edge_i["type90"]))
            dve.sem_inc(types_ready, 1)
            dve.wait_ge(loaded["weights"], 16 * 16)
            link(V.tensor_copy(wa_wide[:], waT[:].unsqueeze(2).to_broadcast([D, 3, P])))
            dve.sem_inc(wide_ready, 1)
            V.tensor_tensor(gate_b[:, 0:2 * D], b_ih[:, 0:2 * D], b_hh[:, 0:2 * D], ALU.add)
            V.tensor_copy(gate_b[:, 2 * D:3 * D], b_ih[:, 2 * D:3 * D])
            link(V.tensor_copy(gate_b[:, 3 * D:4 * D], b_hh[:, 2 * D:3 * D]))

            empty("score_w", lambda b: V.tensor_copy(score_w[:], b[0:D, 0:1]))
            empty("score_wide", lambda b: V.tensor_copy(score_wide[:].rearrange("p k d -> p (k d)"), b[:, 0:3 * D]))
            dve.wait_ge(by_rel_loaded, 16)
            for k, n in enumerate((TYPES, RELS)):
                raw = type_raw[k][:] if k == 0 else type_raw[k][:].rearrange("r (i o) -> r o i", i=D)
                left = type_rest[0:n, :]
                if k == 1:
                    left = left.rearrange("r (o i) -> r o i", i=D)
                part = [type_parts[k][:, m, :] if k == 0 else type_parts[k][:, m, :].rearrange("r (o i) -> r o i", i=D)
                        for m in range(PARTS)]
                link(V.tensor_copy(part[0], raw))
                link(V.tensor_tensor(left, raw, part[0], ALU.subtract))
                link(V.tensor_copy(part[1], left))
                link(V.tensor_tensor(part[2], left, part[1], ALU.subtract))
            dve.wait_ge(filled, fill_no["codes2_1"] + 1)
            dve.wait_ge(loaded["attr"], 48)
            dve.wait_ge(loaded["w"], 48)
            dve.wait_ge(x_loaded, 32)
            dve.sem_inc(taken, 2)
            dve.sem_inc(picked_taken, 2)
            dve.sem_inc(window_taken, 2)

            def tiles_of(b, lo=0, hi=T):
                return bass.ds(b * T + lo, hi - lo)

            def cut_message(layer, b, q, wait_rows, step, between, done):
                gap = [0]

                def link(ins):
                    step.mark(ins)
                    value = step.value()
                    between(gap[0])
                    gap[0] += 1
                    dve.wait_ge(step.sem, value)

                c, d = COLS[layer], 2 * D if layer == 3 else D
                par = parts[:, q, 0:T * c].rearrange("p (t c) -> p t c", t=T)
                msg = got = gathered_rows[:, q, :, 0:D]
                if layer == 0:
                    step.mark(V.memset(par[:, :, c - 1], 1.0))
                if layer == 2:
                    link(V.tensor_tensor(attr_tmp[:], attr[:, tiles_of(b), :],
                                         score_wide[:, 1, :].unsqueeze(1).to_broadcast([P, T, D]), ALU.mult))
                    step.mark(V.tensor_reduce(attr_score[:, tiles_of(b)], attr_tmp[:], AX.X, ALU.add))
                wait_rows()
                if layer == 0:
                    msg = message[:, :, 0:D]
                    link(V.tensor_tensor(msg, got, edge_w[:, tiles_of(b)].unsqueeze(2).to_broadcast([P, T, D]), ALU.mult))
                if layer == 3:
                    msg = message[:]
                    step.mark(V.tensor_tensor(score[:], gathered_rows[:, q, :, D], attr_score[:, tiles_of(b)], ALU.add))
                    link(V.tensor_copy(message[:, :, 0:D], got))
                    link(V.tensor_tensor(message[:, :, D:2 * D], got, score[:].unsqueeze(2).to_broadcast([P, T, D]), ALU.mult))
                link(V.tensor_copy(par[:, :, 0:d], msg))
                link(V.tensor_tensor(rest[:, :, 0:d], msg, par[:, :, 0:d], ALU.subtract))
                dve.sem_inc(taken, 1)
                link(V.tensor_copy(par[:, :, d:2 * d], rest[:, :, 0:d]))
                last = V.tensor_tensor(par[:, :, 2 * d:3 * d], rest[:, :, 0:d], par[:, :, d:2 * d], ALU.subtract)
                if done:
                    last.then_inc(done, 1)
                else:
                    link(last)
                return par

            def loop_of(step, turns, body):
                step.base, step.at = step.base + step.at, 0
                probe = marks_of[body.layer_kind]
                with dve.Fori(0, turns) as i:
                    step.turn = i * probe
                    body(i)
                assert step.at == probe, (body.layer_kind, step.at)
                step.base, step.at, step.turn = step.base + turns * probe, 0, None

            def far_scatter(layer):
                c = COLS[layer]

                def turn(i):
                    for q in range(2):
                        b = i * 2 + q
                        now = b + (layer * BATCHES + 1)
                        dve.wait_ge(ring_ready, now)
                        dve.wait_ge(added, now)
                        for t in range(T):
                            V.tensor_scalar(onehot[:, q, t, :], count[:], code_ring[:, q, t:t + 1], None, ALU.is_equal)
                        par = cut_message(layer, b, q,
                                          lambda: dve.wait_ge(gathered[layer][q], i * (16 * T) + 16 * T), away,
                                          lambda n: None, None)
                        V.tensor_tensor(moving[:, q, 0:T * GROUPS * c].rearrange("p (t a c) -> p t a c", t=T, a=GROUPS),
                                        par.unsqueeze(2).to_broadcast([P, T, GROUPS, c]),
                                        in_group[:, tiles_of(b), :].unsqueeze(3).to_broadcast([P, T, GROUPS, c]),
                                        ALU.mult).then_inc(moving_ready, 1)

                turn.layer_kind = ("far", layer)
                loop_of(away, TURNS, turn)
                dve.wait_ge(sums_ready, layer + 1)
                step_ = away
                d = 2 * D if layer == 3 else D

                def link(ins):
                    step_.mark(ins)
                    dve.wait_ge(step_.sem, step_.value())

                for dst, lo in ((agg, 0), (agg2, D))[:2 if layer == 3 else 1]:
                    link(V.tensor_copy(by_group(dst[:]), part_of(layer, lo)))
                    for k in range(1, PARTS):
                        link(V.tensor_tensor(by_group(dst[:]), by_group(dst[:]), part_of(layer, lo + k * d), ALU.add))
                if layer == 0:
                    counts = sums_of(0)[:, :, 0:GROUPS * COLS[0]].rearrange("p j (a c) -> p j a c", a=GROUPS)[:, :, :, COLS[0] - 1]
                    link(V.tensor_copy(inv_count[:].rearrange("p (a j) -> p j a", j=BLOCKS), counts))
                dve.sem_inc(sums_taken, 1)

            def near_scatter(layer):
                c, by_dma, n = COLS[layer], BY_DMA[layer], PICKS[layer]
                per_load = 16 * CODES[layer]
                loads = sum(16 * k * TURNS for k in CODES[:layer])
                banks = n // HALF
                types = (TYPES, RELS)[layer - 2]

                def link(ins):
                    near.mark(ins)
                    dve.wait_ge(near.sem, near.value())

                def look_up(b, q, turn):
                    dve.wait_ge(code_all_ready[q], turn * per_load + (loads + per_load))
                    if CODES[layer] == 2:
                        V.tensor_scalar(type_lookup[0:types, q, 0:n * P], type_all[0:types, q, 0:n * P],
                                        block_code[0:types, 0:1], None, ALU.is_equal)
                    for j in range(BLOCKS):
                        last = V.tensor_scalar(lookup[:, q, j, 0:n * P], code_all[:, q, 0:n * P], block_code[:, j:j + 1], None, ALU.is_equal)
                    last.then_inc(lookup_ready, 1)

                def windows(b, q, lo=0, hi=T):
                    if lo == 0:
                        dve.wait_ge(ring_ready, b + (layer * BATCHES + 1))
                    for t in range(lo, hi):
                        V.tensor_scalar(near_onehot[:, q, t, :], count[:, 0:P], code_ring[:, q, t:t + 1], None, ALU.is_equal)

                def send(b, q, turn, following):
                    steps = {0: 6, 1: 5, 2: 8, 3: 9}[layer]

                    def some(k):
                        if following:
                            windows(b + 1, 1 - q, k * T // steps, (k + 1) * T // steps)

                    dve.wait_ge(picked, b + (layer * BATCHES + 1))
                    group = in_group[:, tiles_of(b, by_dma), :].rearrange("p t a -> p (t a)")
                    mask = masked[:, 0:n * GD]
                    V.tensor_tensor(mask.rearrange("p (k r d) -> p k r d", k=banks, d=D), picked_rows(layer, q),
                                    group.rearrange("p (k r) -> p k r", k=banks).unsqueeze(3)
                                    .to_broadcast([P, banks, HALF * GROUPS, D]), ALU.mult).then_inc(mask_done, 1)
                    some(0)
                    dve.wait_ge(mask_done, b + (layer * BATCHES + 1))
                    row = gathered_rows[:, q, by_dma:T, 0:D] if layer < 2 else source_x[:]
                    near.mark(V.tensor_reduce(row, mask.rearrange("p (t a d) -> p t d a", t=n, a=GROUPS), AX.X, ALU.add))
                    value = near.value()
                    some(1)
                    dve.wait_ge(near.sem, value)
                    ahead = 2
                    if layer >= 2:
                        near.mark(V.tensor_tensor(product.rearrange("p (t o i) -> p t o i", t=n, o=D),
                                                  matrices(q).rearrange("p (t o i) -> p t o i", t=n, o=D),
                                                  source_x[:].unsqueeze(2).to_broadcast([P, n, D, D]), ALU.mult))
                        value = near.value()
                        if layer == 3:
                            near.mark(V.tensor_tensor(source_tmp[:], source_x[:],
                                                      score_wide[:, 0, :].unsqueeze(1).to_broadcast([P, n, D]), ALU.mult))
                            value = near.value()
                        some(2)
                        dve.wait_ge(near.sem, value)
                        dve.sem_inc(picked_taken, 1)
                        if layer == 3:
                            near.mark(V.tensor_reduce(gathered_rows[:, q, by_dma:T, D], source_tmp[:], AX.X, ALU.add))
                        near.mark(V.tensor_reduce(gathered_rows[:, q, by_dma:T, 0:D].rearrange("p t o -> p t o"),
                                                  product.rearrange("p (t o i) -> p t o i", t=n, o=D), AX.X, ALU.add))
                        value = near.value()
                        some(3)
                        dve.wait_ge(near.sem, value)
                        ahead = 4
                    else:
                        dve.sem_inc(picked_taken, 1)
                    cut_message(layer, b, q, lambda: dve.wait_ge(gathered[layer][q], turn * (16 * by_dma) + 16 * by_dma), near,
                                lambda k: some(ahead + k), moving_ready)

                def add_window(b, q, turn):
                    dve.wait_ge(added, b + (layer * BATCHES + 3))
                    at = bass.ds(turn * STEP2 + q * STEP1, P)
                    V.tensor_tensor(spread[0:c, at], spread[0:c, at], window_sums(q, c), ALU.add).then_inc(window_taken, 1)

                part = [xparts[:, :, k, :].rearrange("p j (a d) -> p j a d", a=GROUPS) for k in range(PARTS)]
                link(V.tensor_copy(part[0], by_group(x)))
                link(V.tensor_tensor(by_group(square[:]), by_group(x), part[0], ALU.subtract))
                link(V.tensor_copy(part[1], by_group(square[:])))
                link(V.tensor_tensor(part[2], by_group(square[:]), part[1], ALU.subtract))
                look_up(0, 0, 0)
                windows(0, 0)
                look_up(1, 1, 0)
                send(0, 0, 0, True)

                def turn(i):
                    look_up(i * 2 + 2, 0, i + 1)
                    add_window(i * 2, 0, i)
                    send(i * 2 + 1, 1, i, True)
                    look_up(i * 2 + 3, 1, i + 1)
                    add_window(i * 2 + 1, 1, i)
                    send(i * 2 + 2, 0, i + 1, True)

                turn.layer_kind = ("near", layer)
                loop_of(near, TURNS - 1, turn)
                add_window(BATCHES - 2, 0, TURNS - 1)
                send(BATCHES - 1, 1, TURNS - 1, False)
                add_window(BATCHES - 1, 1, TURNS - 1)
                dve.wait_ge(window_taken, (layer + 1) * BATCHES + 2)
                dve.sem_inc(spread_ready, 1)
                dve.wait_ge(sums_ready, layer + 1)
                if layer == 3:
                    for k, dst in enumerate((agg, agg2)):
                        for lo, hi in ((0, T), (T, HI)):
                            b = sums[:, 512 * (lo // T):512 * (lo // T) + (hi - lo) * 2 * D]
                            link(V.tensor_copy(dst[:, lo:hi, :], b.rearrange("p (h d) -> p h d", d=2 * D)[:, :, k * D:(k + 1) * D]))
                else:
                    d = D + 1 if layer == 0 else D
                    b = sums[:, 0:HI * d].rearrange("p (h d) -> p h d", d=d)
                    link(V.tensor_copy(agg[:], b[:, :, 0:D]))
                    if layer == 0:
                        link(V.tensor_copy(inv_count[:], b[:, :, D]))
                dve.sem_inc(sums_taken, 1)

            marks_of = {("far", 0): 12, ("far", 1): 8, ("far", 2): 12, ("far", 3): 14,
                        ("near", 0): 12, ("near", 1): 8, ("near", 2): 16, ("near", 3): 22}

            def scatter(layer):
                with dve.If_eq(is_far, 0):
                    near_scatter(layer)
                with dve.Else():
                    far_scatter(layer)

            def wide(t, n=D):
                return t.unsqueeze(1).to_broadcast([P, HI, n])

            def each(t):
                return t.unsqueeze(2).to_broadcast([P, HI, D])

            def norm(layer, ready):
                link(V.tensor_reduce(mean[:], y[:], AX.X, ALU.add))
                link(V.tensor_scalar(mean[:], mean[:], 1.0 / D, None, ALU.mult))
                link(V.tensor_tensor(y[:], y[:], each(mean[:]), ALU.subtract))
                link(V.tensor_tensor(square[:], y[:], y[:], ALU.mult))
                V.tensor_reduce(var[:], square[:], AX.X, ALU.add).then_inc(var_ready, 1)
                dve.wait_ge(std_ready, layer + 1)
                link(V.reciprocal(mean[:], var[:]))
                link(V.tensor_tensor(x, y[:], each(mean[:]), ALU.mult))
                dve.sem_inc(cat_ready, 1)

            scatter(0)
            V.memset(spread[:], 0.0)
            link(V.tensor_scalar(inv_count[:], inv_count[:], 1.0, None, ALU.max))
            link(V.reciprocal(inv_count[:], inv_count[:]))
            link(V.tensor_tensor(agg[:], agg[:], wide(l0_w[:]), ALU.mult))
            link(V.scalar_tensor_tensor(agg[:], x, l0_self[:], agg[:], ALU.mult, ALU.add))
            link(V.tensor_tensor(agg[:], agg[:], x, ALU.add))
            link(V.tensor_scalar(agg[:], agg[:], 0.0, 1.0, ALU.max, ALU.min))
            link(V.tensor_tensor(y[:], agg[:], x, ALU.add))
            norm(0, 1)

            scatter(1)
            link(V.tensor_tensor(cat[:, :, D:2 * D], agg[:], each(inv_count[:]), ALU.mult))
            dve.sem_inc(cat_ready, 1)
            link(V.tensor_tensor(agg[:], x, wide(l1_b[:]), ALU.add))
            empty("l1_linear", lambda b: V.tensor_tensor(y[:].rearrange("p h d -> p (h d)"), b[:, 0:HI * D],
                                                         agg[:].rearrange("p h d -> p (h d)"), ALU.add))
            norm(1, 3)

            dve.wait_ge(table2_saved, 16)
            link(V.memset(spread[:], 0.0))
            scatter(2)
            V.memset(spread[:], 0.0)
            link(V.tensor_copy(cat[:, :, D:2 * D], agg[:]))
            dve.sem_inc(cat_ready, 1)
            for g in range(GATES):
                n = min(8, HI - 8 * g)
                empty(f"l2_gates{g}", lambda b: V.tensor_tensor(
                    gates[:, 8 * g:8 * g + n, :], b[:, 0:n * 4 * D].rearrange("p (h c) -> p h c", h=n),
                    gate_b[:].unsqueeze(1).to_broadcast([P, n, 4 * D]), ALU.add))
            dve.sem_inc(gate_in, 1)
            dve.wait_ge(gate_out, 1)
            link(V.tensor_scalar(gates[:, :, 0:2 * D], gates[:, :, 0:2 * D], 0.5, 0.5, ALU.mult, ALU.add))
            link(V.tensor_tensor(agg[:], gates[:, :, 0:D], gates[:, :, 3 * D:4 * D], ALU.mult))
            V.tensor_tensor(gates[:, :, 2 * D:3 * D], gates[:, :, 2 * D:3 * D], agg[:], ALU.add).then_inc(gate_in, 1)
            dve.wait_ge(gate_out, 2)
            new = gates[:, :, 2 * D:3 * D]
            link(V.tensor_tensor(agg[:], x, new, ALU.subtract))
            link(V.tensor_tensor(agg[:], agg[:], gates[:, :, D:2 * D], ALU.mult))
            link(V.tensor_tensor(agg[:], agg[:], new, ALU.add))
            link(V.tensor_tensor(y[:], agg[:], x, ALU.add))
            dve.wait_ge(wrel_loaded, 16)
            link(V.tensor_copy(wrel[:, :, D:ROW3], score_w[:].unsqueeze(1).to_broadcast([D, RELS, 1])))
            dve.sem_inc(wrel_ready, 1)
            norm(2, 5)
            n = 0
            for h in range(HI):
                if h >= STAGES:
                    dve.wait_ge(table3_saved[h % STAGES], 16 * (h // STAGES))
                for c in (1,) if h % 2 == 0 else (1, 2):
                    name = f"t3_rows{h}_{c}"
                    dve.wait_ge(filled, fill_no[name] + 1)
                    n += 1
                    V.tensor_copy(table3[:, h % STAGES, c * CUT * ROW3:(c + 1) * CUT * ROW3],
                                  bank(name)[:, 0:CUT * ROW3]).then_inc(staged_dve, 1)
                    dve.wait_ge(staged_dve, n)
                    dve.sem_inc(emptied[fill_no[name] % 3], 1)

            scatter(3)
            link(V.tensor_tensor(square[:], x, wide(score_wide[:, 2, :]), ALU.mult))
            link(V.tensor_reduce(mean[:], square[:], AX.X, ALU.add))
            link(V.tensor_tensor(agg[:], agg[:], each(mean[:]), ALU.mult))
            link(V.tensor_tensor(agg[:], agg[:], agg2[:], ALU.add))
            link(V.tensor_tensor(y[:], agg[:], x, ALU.add))
            norm(3, 6)

        @block.tensor
        def _(pe):
            def start(name):
                n = fill_no[name]
                if n >= 3:
                    pe.wait_ge(emptied[n % 3], n // 3)
                return bank(name)

            def transpose(step, rows):
                for g in range(XPOSE):
                    b = start(f"{step}_xpose{g}")
                    for k, h in enumerate(four(g)):
                        last = nc.tensor.transpose(b[0:rows, k * P:(k + 1) * P], cat[:, h, 0:rows], ident[:])
                    last.then_inc(filled, 1)

            def far_scatter(layer):
                c = COLS[layer]
                for b in range(BANKS[layer]):
                    nc.tensor.matmul(sums[:, 512 * b:512 * b + 512], zeros[:, 0:P], zeros[:], start=True, stop=False)
                with pe.Fori(0, TURNS) as i:
                    for q in range(2):
                        pe.wait_ge(moving_ready, i * 2 + (layer * BATCHES + q + 1))
                        mov = moving[:, q, 0:T * GROUPS * c].rearrange("p (t c) -> p t c", t=T)
                        for t in range(T):
                            for j in range(BLOCKS):
                                last = nc.tensor.matmul(sums_of(layer)[:, j, 0:GROUPS * c], onehot[:, q, t, j * P:(j + 1) * P],
                                                        mov[:, t, :], start=False, stop=False, skip_group_check=True)
                        last.then_inc(added, 1)
                for b in range(BANKS[layer]):
                    last = nc.tensor.matmul(sums[:, 512 * b:512 * b + 512], zeros[:, 0:P], zeros[:], start=False, stop=True)
                last.then_inc(sums_ready, 1)

            def near_scatter(layer):
                c, n = COLS[layer], PICKS[layer]

                def pick(b, q):
                    pe.wait_ge(lookup_ready, b + (layer * BATCHES + 1))
                    pe.wait_ge(picked_taken, b + (layer * BATCHES + 1))
                    for t in range(n if layer >= 2 else 0):
                        for k in range(PARTS):
                            types = (TYPES, RELS)[layer - 2]
                            nc.tensor.matmul(matrices(q)[:, t * D * D:(t + 1) * D * D], type_lookup[0:types, q, t * P:(t + 1) * P],
                                             type_parts[layer - 2][:, k, :], start=k == 0, stop=k == PARTS - 1)
                    for t in range(n):
                        at = picked_at(layer, q, t)
                        for j in range(BLOCKS):
                            for k in range(PARTS):
                                last = nc.tensor.matmul(sums[:, at:at + GD], lookup[:, q, j, t * P:(t + 1) * P], xparts[:, j, k, :],
                                                        start=j == 0 and k == 0, stop=j == BLOCKS - 1 and k == PARTS - 1)
                    last.then_inc(picked, 1)

                def add(b, q):
                    pe.wait_ge(moving_ready, b + (layer * BATCHES + 1))
                    pe.wait_ge(window_taken, b + (layer * BATCHES + 1))
                    for t in range(T):
                        last = nc.tensor.matmul(window_sums(q, c), parts[:, q, t * c:(t + 1) * c], near_onehot[:, q, t, :],
                                                start=t == 0, stop=t == T - 1)
                    last.then_inc(added, 1)

                pick(0, 0)
                with pe.Fori(0, TURNS - 1) as i:
                    pick(i * 2 + 1, 1)
                    add(i * 2, 0)
                    pick(i * 2 + 2, 0)
                    add(i * 2 + 1, 1)
                pick(BATCHES - 1, 1)
                add(BATCHES - 2, 0)
                add(BATCHES - 1, 1)
                pe.wait_ge(spread_ready, layer + 1)
                d = {0: D + 1, 3: 2 * D}.get(layer, D)
                f = fold[:] if layer == 3 else fold1[0:c, 0:d]
                for h in range(HI):
                    last = nc.tensor.matmul(folded(h, d), spread[0:c, MARGIN + h * P:MARGIN + (h + 1) * P], f,
                                            start=True, stop=True)
                last.then_inc(sums_ready, 1)

            def scatter(layer):
                if layer:
                    pe.wait_ge(sums_taken, layer)
                with pe.If_eq(is_far, 0):
                    near_scatter(layer)
                with pe.Else():
                    far_scatter(layer)

            pe.wait_ge(const_done, 1)
            pe.sem_inc(added, 2)
            pe.wait_ge(loaded["weights"], 16 * 16)
            nc.tensor.matmul(start("wrel")[0:RELS, 0:D * D], compT[:], bases[:].rearrange("b i o -> b (i o)"),
                             start=True, stop=True).then_inc(filled, 1)
            pe.wait_ge(bounds_ready, 1)
            nc.tensor.matmul(start("bounds")[0:1, 0:1], bounds[:, 1:2], ones[:], start=True, stop=True).then_inc(filled, 1)
            def codes(k, numbers):
                for g in range(2):
                    b = start(f"codes{k}_{g}")
                    for m, t in enumerate(range(4 * g * P, min(4 * (g + 1) * P, TILES), P)):
                        n = min(P, TILES - t)
                        last = nc.tensor.transpose(b[0:n, m * P:(m + 1) * P], numbers[:, t:t + n], ident[:])
                    last.then_inc(filled, 1)

            pe.wait_ge(edges_ready[2], 1)
            codes(0, src_code)
            nc.tensor.matmul(start("score_w")[0:D, 0:1], ws[:], waT[:, 0:1], start=True, stop=True).then_inc(filled, 1)
            b = start("score_wide")
            pe.wait_ge(wide_ready, 1)
            for k in range(3):
                last = nc.tensor.matmul(b[:, k * D:(k + 1) * D], wa_wide[:, k, :], ws[:], start=True, stop=True)
            last.then_inc(filled, 1)

            pe.wait_ge(types_ready, 1)
            codes(1, type_f[0])
            codes(2, type_f[1])
            pe.wait_ge(far_ready, 1)
            is_far = pe.alloc_register("is_far_pe")
            pe.reg_load(is_far, far[0:1, 0:1])
            scatter(0)
            scatter(1)
            pe.wait_ge(cat_ready, 2)
            transpose("l1", 2 * D)
            b = start("l1_linear")
            pe.wait_ge(catT_ready, XPOSE)
            for h in range(HI):
                last = nc.tensor.matmul(b[:, h * D:(h + 1) * D], catT[0:2 * D, h * P:(h + 1) * P], l1_w[:], start=True, stop=True)
            last.then_inc(filled, 1)
            pe.wait_ge(cat_ready, 3)
            transpose("t2", D)
            pe.wait_ge(catT_ready, 2 * XPOSE)
            for g in range(XPOSE):
                b = start(f"t2_rows{g}")
                for k, h in enumerate(four(g)):
                    last = nc.tensor.matmul(b[:, k * P:(k + 1) * P], catT[0:D, h * P:(h + 1) * P],
                                            emb[:].rearrange("i t o -> i (t o)"), start=True, stop=True)
                last.then_inc(filled, 1)
            scatter(2)
            pe.wait_ge(cat_ready, 4)
            transpose("l2", 2 * D)
            pe.wait_ge(catT_ready, 3 * XPOSE)
            for g in range(GATES):
                b = start(f"l2_gates{g}")
                for k, h in enumerate(range(8 * g, min(8 * g + 8, HI))):
                    last = nc.tensor.matmul(b[:, k * 4 * D:(k + 1) * 4 * D], catT[0:2 * D, h * P:(h + 1) * P], gate_w[:],
                                            start=True, stop=True)
                last.then_inc(filled, 1)
            pe.wait_ge(cat_ready, 5)
            transpose("t3", D)
            pe.wait_ge(catT_ready, 4 * XPOSE)
            pe.wait_ge(wrel_ready, 1)
            for h in range(HI):
                for c in range(3):
                    b = start(f"t3_rows{h}_{c}")
                    nc.tensor.matmul(b[:, 0:CUT * ROW3], catT[0:D, h * P:(h + 1) * P],
                                     wrel[:, c * CUT:(c + 1) * CUT, :].rearrange("i r o -> i (r o)"),
                                     start=True, stop=True).then_inc(filled, 1)
            scatter(3)


def kernel(**inputs):
    import numpy as _np
    import concourse.bacc as _bacc
    from concourse import mybir as _mybir
    from concourse.bass_utils import run_bass_kernel_spmd as _run

    nc = _bacc.Bacc("TRN2", target_bir_lowering=False, num_devices=1)
    arrays, given = {}, {}

    def give(name, x):
        x = _np.ascontiguousarray(x)
        arrays[f"in_{name}"] = x
        given[name] = nc.dram_tensor(f"in_{name}", x.shape, _mybir.dt.from_np(x.dtype), kind="ExternalInput").ap()

    for name in ("src", "dst", "edge_type_8", "edge_type_90", "edge_weight", "edge_attr_16"):
        edges = _np.asarray(inputs[name])
        whole, rest = edges[:FULL * P], edges[FULL * P:]
        whole = _np.reshape(whole, (FULL // T, P, T * (edges.size // EDGES)))
        give(name, _np.reshape(_np.transpose(whole, (1, 0, 2)), (P, -1)))
        give(name + "_tail", _np.reshape(rest, (-1,)))
    for name in ("x", "L0_gnn_weight", "L1_gnn_b_l", "L2_gnn_b_ih", "L2_gnn_b_hh", "L2_gnn_edge_emb", "L3_gnn_Ws"):
        give(name, inputs[name])
    give("L0_gnn_self_loop_weight", _np.reshape(inputs["L0_gnn_self_loop_weight"], (1,)))
    give("W_lT", _np.transpose(inputs["L1_gnn_W_l"]))
    give("W_rT", _np.transpose(inputs["L1_gnn_W_r"]))
    give("w_ihT", _np.transpose(inputs["L2_gnn_w_ih"]))
    give("w_hhT", _np.transpose(inputs["L2_gnn_w_hh"]))
    give("L2_gnn_edge_embT", _np.transpose(_np.reshape(inputs["L2_gnn_edge_emb"], (TYPES, D, D)), (2, 0, 1)))
    give("WaT", _np.transpose(_np.reshape(inputs["L3_gnn_Wa"], (3, D))))
    give("w_compT", _np.transpose(inputs["L3_gnn_w_comp"]))
    give("bases", _np.transpose(_np.reshape(inputs["L3_gnn_weight"], (D, BASES, D)), (1, 0, 2)))
    f32 = _mybir.dt.float32
    tables = {
        "wrel": nc.dram_tensor("wrel_flat", (RELS * D * D,), f32).ap(),
        "codes": nc.dram_tensor("edge_codes", (3 * TILES * P,), _mybir.dt.float16).ap(),
        "rows1": nc.dram_tensor("rows1", (PADDED, D), f32).ap(),
        "rows2": nc.dram_tensor("rows2", (PADDED * TYPES, D), f32).ap(),
        "rows3": nc.dram_tensor("rows3", (PADDED * RELS, ROW3), f32).ap(),
    }
    out = nc.dram_tensor("out_0", (NODES, D), f32, kind="ExternalOutput").ap()
    gnn_kernel(nc, given, tables, out)
    r = _run(nc, [arrays], core_ids=[0])
    return r.results[0]["out_0"]
```

```python
import concourse.bass as bass
from concourse import mybir
from contextlib import ExitStack

NODES, EDGES, D = 3125, 103125, 16
P = 128
HI = -(-NODES // P)
GROUPS = 5
BLOCKS = HI // GROUPS
SPAN = BLOCKS * P
PADDED = HI * P
TILES = -(-EDGES // P)
T = 13
FULL = EDGES // (P * T) * T
TAIL = EDGES - FULL * P
BATCHES = TILES // T
TURNS = BATCHES // 2
TYPES, RELS, BASES = 8, 90, 30
PARTS = 3
ROW3 = D + 1
CUT = 30
COLS = [PARTS * D + 1, PARTS * D, PARTS * D, PARTS * 2 * D]
STRIDE = [256, 256, 256, 512]
BANKS = [3, 3, 3, 5]
SCORED = -(-TILES // 7)
ATTR_FIRST = 4 * SCORED
STAGES = 8
EPS = 1e-5
BY_DMA = [(5, 5), (5, 5), (7, 7), (8, 7)]
PICKS = [[T - n for n in by_slot] for by_slot in BY_DMA]
PICKED = max(max(n) for n in PICKS)
TYPED = max(max(n) for n in PICKS[2:])
BY_ACT = [11, 10, T, T]
PICK_BANKS = [2, 2, 1, 1]
PICK_STEP = [128, 128, 80, 80]
CODES = [1, 1, 2, 2]
GD = GROUPS * D
STEP2 = -(-NODES * 2 * P * T // EDGES)
STEP1 = STEP2 // 2
MARGIN = (P - STEP1) // 2
SPREAD = MARGIN + PADDED + 1


class Steps:

    def __init__(self, sem):
        self.sem, self.base, self.at, self.turn = sem, 0, 0, None

    def mark(self, ins):
        ins.then_inc(self.sem, 1)
        self.at += 1

    def value(self):
        return self.base + self.at + (0 if self.turn is None else self.turn)


def gnn_kernel(nc, a, tables, out):
    fp32, bf16, fp16, i32 = mybir.dt.float32, mybir.dt.bfloat16, mybir.dt.float16, mybir.dt.int32
    ALU, ACT, AX = mybir.AluOpType, mybir.ActivationFunctionType, mybir.AxisListType
    assert BATCHES * T == TILES and TURNS * 2 == BATCHES and BLOCKS * GROUPS == HI

    with ExitStack() as ctx:
        def sb(name, shape, dt=fp32):
            return ctx.enter_context(nc.sbuf_tensor(name, shape, dt))

        def sem(name):
            return ctx.enter_context(nc.semaphore(name))

        rows = [sb(f"row_number{k}", [P, TILES]) for k in range(3)]
        code = sb("code", [P, TILES])
        in_group = sb("in_group", [P, TILES, GROUPS], bf16)
        edge_w = sb("edge_w", [P, TILES])
        attr = sb("attr", [P, TILES, D])
        attr_score = sb("attr_score", [P, TILES])
        row_ring = sb("row_ring", [P, 2, T], i32)
        code_ring = sb("code_ring", [P, 2, T])
        gathered_rows = sb("gathered_rows", [P, 2, T, ROW3])
        onehot = sb("onehot", [P, 2, T, BLOCKS * P], bf16)
        moving = sb("moving", [P, 2, T * GROUPS * COLS[3]], bf16)
        score = sb("score", [P, T])
        message = sb("message", [P, T, 2 * D])
        rest = sb("rest", [P, T, 2 * D])
        room = onehot[:].rearrange("p q t c -> p (q t c)")
        names = ("src", "dst", "type8", "type90", "start", "dst_f", "dst_a", "src_a", "src_code", "window")
        first = {n: room[:, 2 * k * TILES:2 * (k + 1) * TILES].bitcast(i32 if k < 5 else fp32) for k, n in enumerate(names)}
        edge_i, starts = first, first["start"]
        dst_f, dst_a, src_a, src_code, window = (first[n] for n in names[5:])
        lookup = room[:, 0:2 * GROUPS * PICKED * P].rearrange("p (q j e) -> p q j e", q=2, j=GROUPS)
        near_onehot = room[:, 2 * GROUPS * PICKED * P:(2 * GROUPS * PICKED + 2 * T) * P].rearrange("p (q t c) -> p q t c", q=2, t=T)
        lookup_typed = room[:, 0:2 * GROUPS * TYPED * P].rearrange("p (q j e) -> p q j e", q=2, j=GROUPS)
        at = 2 * GROUPS * TYPED * P
        near_onehot32 = room[:, at:at + 4 * T * P].bitcast(fp32).rearrange("p (q t c) -> p q t c", q=2, t=T)
        code_all = moving[:, :, 0:PICKED * P].bitcast(fp16)
        masked = moving[:, 0, PICKED * P:PICKED * P + 2 * PICKED * GD].bitcast(fp32)
        at = PICKED * P + 2 * PICKED * GD
        product = moving[:, 0, at:at + 2 * TYPED * D * D].bitcast(fp32)
        type_all = moving[:, 1, PICKED * P:(PICKED + 2 * TYPED) * P].bitcast(fp16).rearrange("p (q e) -> p q e", q=2)
        at = (PICKED + 2 * TYPED) * P
        type_lookup = moving[:, 1, at:at + 2 * TYPED * P].rearrange("p (q e) -> p q e", q=2)
        at += 2 * TYPED * P
        distance = moving[:, 1, at:at + T * P]
        attr_product = moving[:, 0, PICKED * P:PICKED * P + 2 * SCORED * D].bitcast(fp32)
        gates = moving[:, 0, 0:2 * HI * 4 * D].bitcast(fp32).rearrange("p (h c) -> p h c", h=HI)
        at = PICKED * P + 2 * PICKED * GD
        type_f = [moving[:, 0, at + 2 * k * TILES:at + 2 * (k + 1) * TILES].bitcast(fp32) for k in range(2)]
        source_x = sb("source_x", [P, TYPED, D])
        source_tmp = sb("source_tmp", [P, TYPED, D])
        type_raw = [sb("emb_rows", [PARTS * TYPES, D * D]), sb("wrel_by_rel", [RELS, D * D])]
        type_rest = sb("type_rest", [RELS, D * D])
        type_parts = [sb("emb_parts", [PARTS * TYPES, PARTS, D * D], bf16), sb("wrel_parts", [RELS, PARTS, D * D], bf16)]
        emb_stack = sb("emb_stack", [PARTS * TYPES, D * D], bf16)
        type_code = sb("type_code", [P, 1])
        own_part = sb("own_part", [P, PARTS])
        spread = sb("spread", [P, SPREAD])
        xparts = sb("xparts", [P, BLOCKS, PARTS, GD], bf16)
        block_code = sb("block_code", [P, GROUPS])
        bounds = sb("bounds", [P, 2])
        ones = sb("ones", [P, 1])
        far = sb("far", [1, 1], i32)
        parts = sb("parts", [P, 2, T * COLS[3]], bf16)
        cat = sb("cat", [P, HI, 2 * D])
        catT = sb("catT", [P, PADDED])
        blocks = -(-TILES // P)
        codesT = catT[:, 0:3 * blocks * P // 2].bitcast(fp16).rearrange("t (k c p) -> t k c p", k=3, c=blocks)
        agg = sb("agg", [P, HI, D])
        agg2 = sb("agg2", [P, HI, D])
        y = sb("y", [P, HI, D])
        square = sb("square", [P, HI, D])
        mean = sb("mean", [P, HI])
        var = sb("var", [P, HI])
        inv_count = sb("inv_count", [P, HI])
        table2 = spread[:, 0:HI * TYPES * D].rearrange("p (h c) -> p h c", h=HI)
        table3 = attr[:].rearrange("p t d -> p (t d)")[:, 0:STAGES * RELS * ROW3].rearrange("p (s c) -> p s c", s=STAGES)
        diff = sb("diff", [P, P])
        ident = sb("ident", [P, P])
        count_i = sb("count_i", [P, BLOCKS * P], i32)
        count = sb("count", [P, BLOCKS * P], fp16)
        zeros = sb("zeros", [P, 512], bf16)
        eps = sb("eps", [P, 1])
        l0_w = sb("l0_w", [P, D])
        l0_self = sb("l0_self", [P, 1])
        l1_w = sb("l1_w", [2 * D, D])
        l1_b = sb("l1_b", [P, D])
        emb = sb("emb", [D, TYPES, D])
        gate_w = sb("gate_w", [2 * D, 4 * D])
        b_ih = sb("b_ih", [P, 3 * D])
        b_hh = sb("b_hh", [P, 3 * D])
        gate_b = sb("gate_b", [P, 4 * D])
        ws = sb("ws", [D, D])
        waT = sb("waT", [D, 3])
        wa_wide = sb("wa_wide", [D, 3, P])
        score_w = sb("score_w", [D, 1])
        score_wide = sb("score_wide", [P, 3, D])
        bases = sb("bases", [BASES, D, D])
        compT = sb("compT", [BASES, RELS])
        wrel_rows = sb("wrel_rows", [RELS, D * D])
        wrel = sb("wrel", [D, RELS, ROW3])
        wrel_split = moving[0:D, 1, 0:PARTS * RELS * ROW3].rearrange("i (k c) -> i k c", k=PARTS)
        w_parts12 = room[0:2 * PARTS * D, 0:RELS * ROW3]
        w_part3 = room[0:PARTS * D, RELS * ROW3:2 * RELS * ROW3]
        ident_bf = sb("ident_bf", [P, P], bf16)
        x_split = moving[:, 0, 0:HI * 2 * PARTS * D].rearrange("p (h r c) -> p h r c", h=HI, r=2)
        x_splitT = moving[:, 1, 0:PADDED]
        sums = ctx.enter_context(nc.psum_tensor("sums", [P, 5 * 512], fp32))
        nodes = ctx.enter_context(nc.psum_tensor("nodes", [P, 3, 512], fp32))

        cleared = sem("cleared")
        loaded = {n: sem(f"loaded_{n}") for n in ("dst", "src", "w", "types", "attr", "attr_rest", "weights")}
        iota_done = sem("iota_done")
        const_done = sem("const_done")
        x_loaded = sem("x_loaded")
        dve_step = sem("dve_step")
        act_step = sem("act_step")
        edges_ready = [sem(f"edges_ready{k}") for k in range(3)]
        ring_ready = sem("ring_ready")
        gathered = [[sem(f"gathered{k}_{q}") for q in range(2)] for k in range(4)]
        taken = sem("taken")
        moving_ready = sem("moving_ready")
        added = sem("added")
        sums_ready = sem("sums_ready")
        sums_taken = sem("sums_taken")
        filled = sem("filled")
        emptied = [sem(f"emptied{b}") for b in range(3)]
        cat_ready = sem("cat_ready")
        catT_ready = sem("catT_ready")
        var_ready = sem("var_ready")
        std_ready = sem("std_ready")
        gate_in = sem("gate_in")
        gate_out = sem("gate_out")
        wide_ready = sem("wide_ready")
        wrel_out = sem("wrel_out")
        wrel_saved = sem("wrel_saved")
        wrel_loaded = sem("wrel_loaded")
        wrel_ready = sem("wrel_ready")
        wrel_stacked = sem("wrel_stacked")
        table_part = sem("table_part")
        pool_turn = sem("pool_turn")
        staged_act, staged_dve = sem("staged_act"), sem("staged_dve")
        table1_saved, table2_saved = sem("table1_saved"), sem("table2_saved")
        table3_saved = [sem(f"table3_saved{s}") for s in range(STAGES)]
        stored = sem("stored")
        starts_done = sem("starts_done")
        bounds_ready = sem("bounds_ready")
        far_ready = sem("far_ready")
        codesT_part = sem("codesT_part")
        codes_saved = [sem(f"codes_saved{k}") for k in range(3)]
        code_all_ready = [sem(f"code_all_ready{q}") for q in range(2)]
        types_ready = sem("types_ready")
        by_rel_loaded = sem("by_rel_loaded")
        windows_ready = sem("windows_ready")
        near_act_step = sem("near_act_step")
        matrices_ready = sem("matrices_ready")
        matrices_taken = sem("matrices_taken")
        lookup_ready = sem("lookup_ready")
        picked = sem("picked")
        picked_taken = sem("picked_taken")
        window_taken = sem("window_taken")
        spread_ready = sem("spread_ready")
        near_step = sem("near_step")
        far_step = sem("far_step")

        def sums_of(layer):
            return sums[:, 0:BLOCKS * STRIDE[layer]].rearrange("p (j c) -> p j c", j=BLOCKS)

        def by_group(t):
            return t.rearrange("p (a j) d -> p j a d", j=BLOCKS)

        def part_of(layer, lo):
            c = COLS[layer]
            return sums_of(layer)[:, :, 0:GROUPS * c].rearrange("p j (a c) -> p j a c", a=GROUPS)[:, :, :, lo:lo + D]

        x = cat[:, :, 0:D]

        XPOSE = -(-HI // 4)
        GATES = -(-HI // 8)
        order = ["wrel", "bounds", "codes0_0", "codes0_1", "score_w", "score_wide", "codes1_0", "codes1_1", "codes2_0", "codes2_1"]
        order += [f"l1_xpose{g}" for g in range(XPOSE)] + ["l1_linear"]
        order += [f"t2_xpose{g}" for g in range(XPOSE)] + [f"t2_rows{g}" for g in range(XPOSE)]
        order += [f"l2_xpose{g}" for g in range(XPOSE)] + [f"l2_gates{g}" for g in range(GATES)]
        order += [f"t3_xpose{g}" for g in range(XPOSE)] + [f"t3_rows{h}_{c}" for h in range(HI) for c in range(3)]
        fill_no = {n: k for k, n in enumerate(order)}

        def picked_rows(layer, q):
            at, n, step = 512 * PICK_BANKS[layer] * q, PICKS[layer][q], PICK_STEP[layer]
            return sums[:, at:at + n * step].rearrange("p (t c) -> p t c", t=n)[:, :, 0:GD]

        matrices = sums[:, 1024:1024 + TYPED * D * D]

        def lookup_of(layer):
            return lookup if layer < 2 else lookup_typed

        def windows_of(layer):
            return near_onehot if layer < 2 else near_onehot32

        def near_width(layer):
            return (COLS[0], COLS[1], D, 2 * D)[layer]

        def message32(layer, q):
            d = near_width(layer)
            return parts[:, q, 0:2 * T * d].bitcast(fp32).rearrange("p (t d) -> p t d", t=T)

        def window_sums(q, c):
            return nodes[0:c, q, 0:P]

        def turned(c):
            return sums[:].rearrange("p (b c) -> p b c", b=5)[:, :, 0:5 * c].rearrange("p b (h c) -> p b h c", h=5)

        def bank(name):
            return nodes[:, fill_no[name] % 3, :]

        def four(g):
            return range(4 * g, min(4 * g + 4, HI))

        block = ctx.enter_context(nc.Block())

        @block.sync
        def _(sp):
            def load_edges(tile, name, s, width=1, lo=0):
                sp.dma_start(tile[:, lo:FULL * width], a[name][:, lo:FULL * width]).then_inc(s, 16)
                whole = TAIL // T
                sp.dma_start(tile[0:whole, FULL * width:TILES * width],
                             a[name + "_tail"][0:whole * T * width].rearrange("(p t) -> p t", p=whole)).then_inc(s, 16)
                sp.dma_start(tile[whole:whole + 1, FULL * width:(FULL + TAIL - whole * T) * width],
                             a[name + "_tail"][whole * T * width:TAIL * width].rearrange("(p t) -> p t", p=1)).then_inc(s, 16)

            sp.wait_ge(cleared, 1)
            load_edges(edge_i["src"], "src", loaded["src"])
            load_edges(edge_i["dst"], "dst", loaded["dst"])
            load_edges(edge_w, "edge_weight", loaded["w"])
            full = NODES // P
            sp.dma_start(cat[:, 0:full, 0:D], a["x"][0:full * P, :].rearrange("(h p) d -> p h d", p=P)).then_inc(x_loaded, 16)
            sp.dma_start(cat[0:NODES - full * P, full, 0:D], a["x"][full * P:NODES, :]).then_inc(x_loaded, 16)
            w = [(l0_w[:], a["L0_gnn_weight"].partition_broadcast(P)),
                 (l0_self[:], a["L0_gnn_self_loop_weight"].partition_broadcast(P)),
                 (l1_w[0:D, :], a["W_rT"]), (l1_w[D:2 * D, :], a["W_lT"]),
                 (l1_b[:], a["L1_gnn_b_l"].partition_broadcast(P)),
                 (emb[:], a["L2_gnn_edge_embT"]),
                 (gate_w[0:D, 0:2 * D], a["w_hhT"][:, 0:2 * D]), (gate_w[0:D, 3 * D:4 * D], a["w_hhT"][:, 2 * D:3 * D]),
                 (gate_w[D:2 * D, 0:3 * D], a["w_ihT"]),
                 (b_ih[:], a["L2_gnn_b_ih"].partition_broadcast(P)), (b_hh[:], a["L2_gnn_b_hh"].partition_broadcast(P)),
                 *[(type_raw[0][k * TYPES:(k + 1) * TYPES, :], a["L2_gnn_edge_emb"]) for k in range(PARTS)],
                 (ws[:], a["L3_gnn_Ws"]), (waT[:], a["WaT"]), (compT[:], a["w_compT"]), (bases[:], a["bases"])]
            for dst, src in w:
                sp.dma_start(dst, src).then_inc(loaded["weights"], 16)
            load_edges(edge_i["type8"], "edge_type_8", loaded["types"])
            load_edges(edge_i["type90"], "edge_type_90", loaded["types"])
            whole = TILES // P

            def save_codes(k):
                sp.wait_ge(codesT_part, 2 * (k + 1))
                codes = tables["codes"][k * TILES * P:(k + 1) * TILES * P].rearrange("(t p) -> t p", p=P)
                sp.dma_start(codes[0:whole * P, :].rearrange("(c t) p -> t c p", t=P), codesT[:, k, 0:whole, :]).then_inc(codes_saved[k], 16)
                sp.dma_start(codes[whole * P:TILES, :], codesT[0:TILES - whole * P, k, whole, :]).then_inc(codes_saved[k], 16)

            save_codes(0)
            sp.wait_ge(codes_saved[0], 32)
            sp.wait_ge(far_ready, 1)
            is_far = sp.alloc_register("is_far_sp")
            sp.reg_load(is_far, far[0:1, 0:1])

            def send(layer, b, q):
                n = PICKS[layer][q] * P
                at = b * (T * P) + BY_DMA[layer][q] * P
                sp.dma_start(code_all[:, q, 0:n], tables["codes"][bass.ds(at, n)].partition_broadcast(P)).then_inc(code_all_ready[q], 16)
                if CODES[layer] == 2:
                    at = at + (layer - 1) * TILES * P
                    sp.dma_start(type_all[:, q, 0:n], tables["codes"][bass.ds(at, n)].partition_broadcast(P)).then_inc(code_all_ready[q], 16)

            def send_first(layer):
                if layer:
                    sp.wait_ge(lookup_ready, layer * BATCHES)
                send(layer, 0, 0)
                send(layer, 1, 1)

            def send_rest(layer):
                with sp.Fori(0, TURNS - 1) as i:
                    for q in range(2):
                        sp.wait_ge(lookup_ready, i * 2 + (layer * BATCHES + q + 1))
                        send(layer, i * 2 + 2 + q, q)

            def send_codes(layer):
                send_first(layer)
                send_rest(layer)

            with sp.If_eq(is_far, 0):
                send_first(0)
            some, all_attr = ATTR_FIRST * D, attr[:].rearrange("p t d -> p (t d)")
            sp.dma_start(all_attr[:, 0:some], a["edge_attr_16"][:, 0:some]).then_inc(loaded["attr"], 16)
            save_codes(1)
            save_codes(2)
            with sp.If_eq(is_far, 0):
                send_rest(0)
            load_edges(all_attr, "edge_attr_16", loaded["attr_rest"], D, some)
            sp.wait_ge(wrel_out, 1)
            sp.dma_start(tables["wrel"].rearrange("(i r o) -> r i o", i=D, r=RELS),
                         wrel_rows[:].rearrange("r (i o) -> r i o", i=D)).then_inc(wrel_saved, 16)
            sp.wait_ge(wrel_saved, 16)
            sp.dma_start(wrel[:, :, 0:D], tables["wrel"].rearrange("(r i o) -> i r o", r=RELS, i=D)).then_inc(wrel_loaded, 16)

            sp.dma_start(type_raw[1][:], tables["wrel"].rearrange("(r c) -> r c", r=RELS)).then_inc(by_rel_loaded, 16)
            sp.wait_ge(cat_ready, 1)
            sp.dma_start(tables["rows1"].rearrange("(h p) d -> p h d", p=P), x).then_inc(table1_saved, 16)
            with sp.If_eq(is_far, 0):
                send_codes(1)
            for k in (1, 2):
                sp.wait_ge(codes_saved[k], 32)
            rows2 = tables["rows2"].rearrange("(h p t) d -> p h (t d)", p=P, t=TYPES)
            for g in range(XPOSE):
                blocks = slice(4 * g, 4 * g + len(four(g)))
                sp.wait_ge(table_part, g + 1)
                sp.dma_start(rows2[:, blocks, :], table2[:, blocks, :]).then_inc(table2_saved, 16)
            with sp.If_eq(is_far, 0):
                send_codes(2)
            sp.wait_ge(wrel_ready, 1)
            for k in range(PARTS):
                for part in range(2):
                    at = (part * PARTS + k) * D
                    sp.dma_start(w_parts12[at:at + D, :], wrel_split[:, part, :]).then_inc(wrel_stacked, 16)
                sp.dma_start(w_part3[k * D:(k + 1) * D, :], wrel_split[:, 2, :]).then_inc(wrel_stacked, 16)
            rows3 = tables["rows3"].rearrange("(h p r) d -> h p (r d)", p=P, r=RELS)
            for h in range(HI):
                sp.wait_ge(staged_act, h + 1 + (h + 2) // 2)
                sp.wait_ge(staged_dve, h + 1 + (h + 1) // 2)
                sp.dma_start(rows3[h], table3[:, h % STAGES, :]).then_inc(table3_saved[h % STAGES], 16)
            with sp.If_eq(is_far, 0):
                send_codes(3)
            sp.wait_ge(cat_ready, 6)
            sp.dma_start(out[0:full * P, :].rearrange("(h p) d -> p h d", p=P), cat[:, 0:full, 0:D]).then_inc(stored, 16)
            sp.dma_start(out[full * P:NODES, :], cat[0:NODES - full * P, full, 0:D]).then_inc(stored, 16)
            sp.wait_ge(stored, 32)

        @block.gpsimd
        def _(pool):
            nc.gpsimd.iota(count_i[:], pattern=[[1, BLOCKS * P]], base=0, channel_multiplier=0).then_inc(iota_done, 1)
            nc.gpsimd.iota(diff[:], pattern=[[1, P]], base=0, channel_multiplier=-1,
                           allow_small_or_imprecise_dtypes=True).then_inc(iota_done, 1)
            nc.gpsimd.iota(starts, pattern=[[STEP2, TURNS], [STEP1, 2], [0, T]], base=-MARGIN,
                           channel_multiplier=0).then_inc(starts_done, 1)
            pool.wait_ge(far_ready, 1)
            is_far = pool.alloc_register("is_far_pool")
            pool.reg_load(is_far, far[0:1, 0:1])

            def gather(layer, tiles, near):
                table = (a["x"], tables["rows1"], tables["rows2"], tables["rows3"])[layer]
                width = ROW3 if layer == 3 else D
                with pool.Fori(0, TURNS) as i:
                    for q in range(2):
                        pool.wait_ge(ring_ready, i * 2 + (layer * BATCHES + q + 1))
                        if near:
                            pool.wait_ge(taken, i * 2 + (layer * BATCHES + q + 1))
                        pool.sem_inc(pool_turn, 1)
                        for t in range(tiles[q]):
                            nc.gpsimd.indirect_dma_start(
                                gathered_rows[:, q, t, 0:width], None, table,
                                bass.IndirectOffsetOnAxis(row_ring[:, q, t:t + 1], 0)).then_inc(gathered[layer][q], 16)

            for layer in range(4):
                if layer == 1:
                    pool.wait_ge(table1_saved, 16)
                if layer == 2:
                    pool.wait_ge(table2_saved, 16 * XPOSE)
                if layer == 3:
                    for s in range(STAGES):
                        pool.wait_ge(table3_saved[s], 16 * len(range(s, HI, STAGES)))
                with pool.If_eq(is_far, 0):
                    gather(layer, BY_DMA[layer], True)
                with pool.Else():
                    gather(layer, (T, T), False)

        @block.scalar
        def _(act):
            def evacuate(name, dst, src, done, value):
                act.wait_ge(filled, fill_no[name] + 1)
                nc.scalar.copy(dst, src).then_inc(done, 1)
                act.wait_ge(done, value)
                act.sem_inc(emptied[fill_no[name] % 3], 1)

            def transpose_out(step, rows, base):
                for g in range(XPOSE):
                    n = 128 * len(four(g))
                    evacuate(f"{step}_xpose{g}", catT[0:rows, 512 * g:512 * g + n],
                             bank(f"{step}_xpose{g}")[0:rows, 0:n], catT_ready, base + g + 1)

            near = Steps(near_act_step)

            def near_feed(layer):
                numbers = rows[max(0, layer - 1)]

                def fill(b, q):
                    near.mark(nc.scalar.copy(row_ring[:, q, :], numbers[:, bass.ds(b * T, T)]))
                    near.mark(nc.scalar.copy(code_ring[:, q, :], code[:, bass.ds(b * T, T)]))
                    act.wait_ge(near.sem, near.value())
                    act.sem_inc(ring_ready, 1)

                def windows(b, q):
                    act.wait_ge(added, b + (layer * BATCHES + 1))
                    n = BY_ACT[layer]
                    for t in range(n):
                        last = nc.scalar.activation(distance[:, t * P:(t + 1) * P], count[:, 0:P], ACT.Abs,
                                                    bias=code_ring[:, q, t:t + 1], scale=-1.0)
                    near.mark(last)
                    act.wait_ge(near.sem, near.value())
                    nc.scalar.activation(windows_of(layer)[:, q, 0:n, :].rearrange("p t c -> p (t c)"), distance[:, 0:n * P], ACT.Relu,
                                         bias=1.0, scale=-1.0).then_inc(windows_ready, 1)

                fill(0, 0)
                windows(0, 0)
                fill(1, 1)
                near.base, near.at = near.base + near.at, 0
                with act.Fori(0, TURNS - 1) as i:
                    near.turn = i * 6
                    for q in range(2):
                        act.wait_ge(gathered[layer][q], i * (16 * BY_DMA[layer][q]) + 16 * BY_DMA[layer][q])
                        fill(i * 2 + 2 + q, q)
                        windows(i * 2 + 1 + q, 1 - q)
                assert near.at == 6
                near.base, near.at, near.turn = near.base + 6 * (TURNS - 1), 0, None
                act.wait_ge(windows_ready, (layer + 1) * BATCHES - 1)
                windows(BATCHES - 1, 1)

            def feed(layer):
                with act.If_eq(is_far, 0):
                    near_feed(layer)
                with act.Else():
                    far_feed(layer)

            def far_feed(layer):
                numbers = rows[max(0, layer - 1)]
                with act.Fori(0, TURNS) as i:
                    for q in range(2):
                        act.wait_ge(taken, i * 2 + (layer * BATCHES + q + 1))
                        nc.scalar.copy(row_ring[:, q, :], numbers[:, bass.ds(i * (2 * T) + q * T, T)]).then_inc(act_step, 1)
                        nc.scalar.copy(code_ring[:, q, :], code[:, bass.ds(i * (2 * T) + q * T, T)]).then_inc(act_step, 1)
                        act.wait_ge(act_step, i * 4 + (layer * 2 * BATCHES + 2 * q + 2))
                        act.sem_inc(ring_ready, 1)

            def root(k):
                act.wait_ge(var_ready, k)
                nc.scalar.activation(var[:], var[:], ACT.Sqrt, bias=eps[:], scale=1.0 / D).then_inc(std_ready, 1)

            evacuate("wrel", wrel_rows[:], bank("wrel")[0:RELS, 0:D * D], wrel_out, 1)
            def codes_out(k):
                last, n = TILES % P, -(-TILES // P) - 5
                evacuate(f"codes{k}_0", codesT[:, k, 0:4, :].rearrange("t c p -> t (c p)"), bank(f"codes{k}_0"), codesT_part, 2 * k + 1)
                b = bank(f"codes{k}_1")
                act.wait_ge(filled, fill_no[f"codes{k}_1"] + 1)
                nc.scalar.copy(codesT[:, k, 4:4 + n, :].rearrange("t c p -> t (c p)"), b[:, 0:n * P])
                nc.scalar.copy(codesT[0:last, k, 4 + n, :], b[0:last, n * P:(n + 1) * P]).then_inc(codesT_part, 1)
                act.wait_ge(codesT_part, 2 * k + 2)
                act.sem_inc(emptied[fill_no[f"codes{k}_1"] % 3], 1)

            for k in range(3):
                codes_out(k)
            act.wait_ge(far_ready, 1)
            is_far = act.alloc_register("is_far_act")
            act.reg_load(is_far, far[0:1, 0:1])
            act.wait_ge(edges_ready[0], 1)
            feed(0)
            root(1)
            act.wait_ge(edges_ready[1], 1)
            feed(1)
            transpose_out("l1", 2 * D, 0)
            root(2)
            transpose_out("t2", D, XPOSE)
            for g in range(XPOSE):
                n = len(four(g))
                evacuate(f"t2_rows{g}", table2[:, 4 * g:4 * g + n, :].rearrange("p h c -> p (h c)"),
                         bank(f"t2_rows{g}")[:, 0:n * P], table_part, g + 1)
            feed(2)
            transpose_out("l2", 2 * D, 2 * XPOSE)
            act.wait_ge(gate_in, 1)
            nc.scalar.activation(gates[:, :, 0:2 * D], gates[:, :, 0:2 * D], ACT.Tanh, scale=0.5).then_inc(gate_out, 1)
            act.wait_ge(gate_in, 2)
            nc.scalar.activation(gates[:, :, 2 * D:3 * D], gates[:, :, 2 * D:3 * D], ACT.Tanh).then_inc(gate_out, 1)
            root(3)
            act.wait_ge(wrel_stacked, 16 * 3 * PARTS)
            for g in range(XPOSE):
                n = P * len(four(g))
                evacuate(f"t3_xpose{g}", x_splitT[0:2 * PARTS * D, 512 * g:512 * g + n],
                         bank(f"t3_xpose{g}")[0:2 * PARTS * D, 0:n], catT_ready, 3 * XPOSE + g + 1)
            n = 0
            for h in range(HI):
                if h >= STAGES:
                    act.wait_ge(table3_saved[h % STAGES], 16 * (h // STAGES))
                for c in range(h % 2, 3, 2):
                    n += 1
                    evacuate(f"t3_rows{h}_{c}", table3[:, h % STAGES, c * CUT * ROW3:(c + 1) * CUT * ROW3],
                             bank(f"t3_rows{h}_{c}")[:, 0:CUT * ROW3], staged_act, n)
            feed(3)
            root(4)

        @block.vector
        def _(dve):
            step = Steps(dve_step)

            def link(ins):
                step.mark(ins)
                dve.wait_ge(step.sem, step.value())

            V = nc.vector
            for n in ("src", "type8", "type90"):
                V.memset(edge_i[n][96:P, FULL:TILES], 0)
            V.memset(edge_i["dst"][96:P, FULL:TILES], NODES)
            V.memset(edge_w[96:P, FULL:TILES], 0.0)
            V.memset(attr[96:P, FULL:TILES, :], 0.0)
            V.memset(cat[:], 0.0)
            link(V.memset(gate_w[:], 0.0))
            dve.sem_inc(cleared, 1)
            V.memset(zeros[:], 0.0)
            V.memset(ones[:], 1.0)
            V.memset(eps[:], EPS)
            dve.wait_ge(iota_done, 2)
            V.tensor_copy(count[:], count_i[:])
            for j in range(BLOCKS):
                V.tensor_scalar(block_code[:, j:j + 1], diff[:, 0:1], -1.0, float(P * j), ALU.mult, ALU.add)
            V.tensor_scalar(ident_bf[:], diff[:], 0.0, None, ALU.is_equal)
            link(V.tensor_scalar(ident[:], diff[:], 0.0, None, ALU.is_equal))
            dve.sem_inc(const_done, 1)
            dve.wait_ge(loaded["dst"], 48)
            link(V.tensor_copy(dst_f, edge_i["dst"]))
            dve.wait_ge(starts_done, 1)
            link(V.tensor_tensor(window, dst_f, starts, ALU.subtract))
            V.tensor_reduce(bounds[:, 0:1], window, AX.X, ALU.max)
            link(V.tensor_reduce(bounds[:, 1:2], window, AX.X, ALU.min))
            link(V.tensor_scalar(bounds[:, 0:1], bounds[:, 0:1], float(P), None, ALU.is_ge))
            link(V.scalar_tensor_tensor(bounds[:, 1:2], bounds[:, 1:2], 0.0, bounds[:, 0:1], ALU.is_lt, ALU.add))
            dve.sem_inc(bounds_ready, 1)

            def split_by_span(f, group, rest):
                link(V.tensor_scalar(group, f, float(SPAN), None, ALU.is_ge))
                for k in range(2, GROUPS):
                    link(V.scalar_tensor_tensor(group, f, float(SPAN * k), group, ALU.is_ge, ALU.add))
                link(V.scalar_tensor_tensor(rest, group, -float(SPAN), f, ALU.mult, ALU.add))

            dve.wait_ge(loaded["src"], 48)
            link(V.tensor_copy(rows[0][:], edge_i["src"]))
            split_by_span(rows[0][:], src_a, src_code)
            dve.sem_inc(edges_ready[2], 1)
            split_by_span(dst_f, dst_a, code[:])

            def empty(name, ins_of):
                dve.wait_ge(filled, fill_no[name] + 1)
                link(ins_of(bank(name)))
                dve.sem_inc(emptied[fill_no[name] % 3], 1)

            empty("bounds", lambda b: V.tensor_copy(far[:], b[0:1, 0:1]))
            dve.sem_inc(far_ready, 1)
            is_far = dve.alloc_register("is_far_dve")
            dve.reg_load(is_far, far[0:1, 0:1])
            near, away = Steps(near_step), Steps(far_step)
            with dve.If_eq(is_far, 0):
                V.tensor_copy(code[:], window)
                for k in range(GROUPS):
                    V.tensor_scalar(in_group[:, :, k], src_a, float(k), None, ALU.is_equal)
            with dve.Else():
                for k in range(GROUPS):
                    V.tensor_scalar(in_group[:, :, k], dst_a, float(k), None, ALU.is_equal)
            link(V.tensor_copy(score[:, 0:1], eps[:]))
            dve.sem_inc(edges_ready[0], 1)
            dve.wait_ge(loaded["types"], 96)
            V.scalar_tensor_tensor(rows[1][:], rows[0][:], float(TYPES), edge_i["type8"], ALU.mult, ALU.add)
            link(V.scalar_tensor_tensor(rows[2][:], rows[0][:], float(RELS), edge_i["type90"], ALU.mult, ALU.add))
            dve.sem_inc(edges_ready[1], 1)
            V.tensor_copy(type_f[0], edge_i["type8"])
            link(V.tensor_copy(type_f[1], edge_i["type90"]))
            dve.sem_inc(types_ready, 1)
            part_no = own_part[:, 0:1]
            link(V.tensor_scalar(own_part[:, 1:2], block_code[:, 0:1], float(TYPES), None, ALU.is_ge))
            link(V.tensor_scalar(own_part[:, 2:3], block_code[:, 0:1], float(2 * TYPES), None, ALU.is_ge))
            link(V.tensor_tensor(part_no, own_part[:, 1:2], own_part[:, 2:3], ALU.add))
            V.scalar_tensor_tensor(type_code[:], part_no, -float(TYPES), block_code[:, 0:1], ALU.mult, ALU.add)
            link(V.tensor_tensor(own_part[:, 1:2], own_part[:, 1:2], own_part[:, 2:3], ALU.subtract))
            link(V.tensor_scalar(part_no, part_no, 0.0, None, ALU.is_equal))
            dve.wait_ge(loaded["weights"], 16 * 18)
            link(V.tensor_copy(wa_wide[:], waT[:].unsqueeze(2).to_broadcast([D, 3, P])))
            dve.sem_inc(wide_ready, 1)
            V.tensor_tensor(gate_b[:, 0:2 * D], b_ih[:, 0:2 * D], b_hh[:, 0:2 * D], ALU.add)
            V.tensor_copy(gate_b[:, 2 * D:3 * D], b_ih[:, 2 * D:3 * D])
            link(V.tensor_copy(gate_b[:, 3 * D:4 * D], b_hh[:, 2 * D:3 * D]))

            empty("score_w", lambda b: V.tensor_copy(score_w[:], b[0:D, 0:1]))
            empty("score_wide", lambda b: V.tensor_copy(score_wide[:].rearrange("p k d -> p (k d)"), b[:, 0:3 * D]))
            dve.wait_ge(filled, fill_no["codes2_1"] + 1)
            dve.wait_ge(loaded["w"], 48)
            dve.wait_ge(x_loaded, 32)
            dve.sem_inc(taken, 2)
            dve.sem_inc(picked_taken, 2)
            dve.sem_inc(matrices_taken, 1)
            dve.sem_inc(window_taken, 2)

            def tiles_of(b, lo=0, hi=T):
                return bass.ds(b * T + lo, hi - lo)

            CHUNKS = [range(0, 1), range(1, 2), (), ()]

            def own_scores(chunks, step):
                for k in chunks:
                    dve.wait_ge(loaded["attr"], 16)
                    if (k + 1) * SCORED > ATTR_FIRST:
                        dve.wait_ge(loaded["attr_rest"], 48)
                    n = min(SCORED, TILES - k * SCORED)
                    tiles = slice(k * SCORED, k * SCORED + n)
                    product = attr_product[:, 0:n * D].rearrange("p (t d) -> p t d", d=D)
                    for ins in (lambda: V.tensor_tensor(product, attr[:, tiles, :],
                                                        score_wide[:, 1, :].unsqueeze(1).to_broadcast([P, n, D]), ALU.mult),
                                lambda: V.tensor_reduce(attr_score[:, tiles], product, AX.X, ALU.add)):
                        step.mark(ins())
                        dve.wait_ge(step.sem, step.value())

            def cut_message(layer, b, q, wait_rows, step, between, done):
                gap = [0]

                def link(ins):
                    step.mark(ins)
                    value = step.value()
                    between(gap[0])
                    gap[0] += 1
                    dve.wait_ge(step.sem, value)

                c, d = COLS[layer], 2 * D if layer == 3 else D
                par = parts[:, q, 0:T * c].rearrange("p (t c) -> p t c", t=T)
                msg = got = gathered_rows[:, q, :, 0:D]
                wait_rows()
                if layer == 0:
                    msg = message[:, :, 0:D]
                    link(V.tensor_tensor(msg, got, edge_w[:, tiles_of(b)].unsqueeze(2).to_broadcast([P, T, D]), ALU.mult))
                if layer == 3:
                    msg = message[:]
                    step.mark(V.tensor_tensor(score[:], gathered_rows[:, q, :, D], attr_score[:, tiles_of(b)], ALU.add))
                    link(V.tensor_copy(message[:, :, 0:D], got))
                    link(V.tensor_tensor(message[:, :, D:2 * D], got, score[:].unsqueeze(2).to_broadcast([P, T, D]), ALU.mult))
                link(V.tensor_copy(par[:, :, 0:d], msg))
                link(V.tensor_tensor(rest[:, :, 0:d], msg, par[:, :, 0:d], ALU.subtract))
                dve.sem_inc(taken, 1)
                link(V.tensor_copy(par[:, :, d:2 * d], rest[:, :, 0:d]))
                last = V.tensor_tensor(par[:, :, 2 * d:3 * d], rest[:, :, 0:d], par[:, :, d:2 * d], ALU.subtract)
                if done:
                    last.then_inc(done, 1)
                else:
                    link(last)
                return par

            def count_column():
                for q in range(2):
                    V.memset(parts[:, q, 0:T * COLS[0]].rearrange("p (t c) -> p t c", t=T)[:, :, COLS[0] - 1], 1.0)

            def loop_of(step, turns, body):
                step.base, step.at = step.base + step.at, 0
                probe = marks_of[body.layer_kind]
                with dve.Fori(0, turns) as i:
                    step.turn = i * probe
                    body(i)
                assert step.at == probe, (body.layer_kind, step.at)
                step.base, step.at, step.turn = step.base + turns * probe, 0, None

            def far_scatter(layer):
                c = COLS[layer]

                def turn(i):
                    for q in range(2):
                        b = i * 2 + q
                        now = b + (layer * BATCHES + 1)
                        dve.wait_ge(ring_ready, now)
                        dve.wait_ge(added, now)
                        for t in range(T):
                            V.tensor_scalar(onehot[:, q, t, :], count[:], code_ring[:, q, t:t + 1], None, ALU.is_equal)
                        par = cut_message(layer, b, q,
                                          lambda: dve.wait_ge(gathered[layer][q], i * (16 * T) + 16 * T), away,
                                          lambda n: None, None)
                        V.tensor_tensor(moving[:, q, 0:T * GROUPS * c].rearrange("p (t a c) -> p t a c", t=T, a=GROUPS),
                                        par.unsqueeze(2).to_broadcast([P, T, GROUPS, c]),
                                        in_group[:, tiles_of(b), :].unsqueeze(3).to_broadcast([P, T, GROUPS, c]),
                                        ALU.mult).then_inc(moving_ready, 1)

                if layer == 0:
                    count_column()
                turn.layer_kind = ("far", layer)
                loop_of(away, TURNS, turn)
                dve.wait_ge(sums_ready, layer + 1)
                own_scores(CHUNKS[layer], away)
                d = 2 * D if layer == 3 else D

                def link(ins):
                    away.mark(ins)
                    dve.wait_ge(away.sem, away.value())

                for dst, lo in ((agg, 0), (agg2, D))[:2 if layer == 3 else 1]:
                    link(V.tensor_copy(by_group(dst[:]), part_of(layer, lo)))
                    for k in range(1, PARTS):
                        link(V.tensor_tensor(by_group(dst[:]), by_group(dst[:]), part_of(layer, lo + k * d), ALU.add))
                if layer == 0:
                    counts = sums_of(0)[:, :, 0:GROUPS * COLS[0]].rearrange("p j (a c) -> p j a c", a=GROUPS)[:, :, :, COLS[0] - 1]
                    link(V.tensor_copy(inv_count[:].rearrange("p (a j) -> p j a", j=BLOCKS), counts))
                dve.sem_inc(sums_taken, 1)

            def near_scatter(layer):
                c = near_width(layer)
                per_load = 16 * CODES[layer]
                loads = sum(16 * k * TURNS for k in CODES[:layer])
                types = (PARTS * TYPES, RELS)[layer - 2]
                lookups = BLOCKS + CODES[layer] - 1
                by_act = BY_ACT[layer]
                gaps = {0: 6, 1: 5, 2: 5, 3: 5}[layer]

                def link(ins):
                    near.mark(ins)
                    dve.wait_ge(near.sem, near.value())

                def look_up(b, q, turn, lo=0, hi=lookups):
                    if lo == 0 and hi:
                        dve.wait_ge(code_all_ready[q], turn * per_load + (loads + per_load))
                    n = PICKS[layer][q]
                    for k in range(lo, hi):
                        if k < BLOCKS:
                            last = V.tensor_scalar(lookup_of(layer)[:, q, k, 0:n * P], code_all[:, q, 0:n * P],
                                                   block_code[:, k:k + 1], None, ALU.is_equal)
                        else:
                            last = V.tensor_scalar(type_lookup[0:types, q, 0:n * P], type_all[0:types, q, 0:n * P],
                                                   (type_code if layer == 2 else block_code)[0:types, 0:1], None, ALU.is_equal)
                        if k == lookups - 1:
                            last.then_inc(lookup_ready, 1)

                def send(b, q, turn, following):
                    def some(k):
                        if k == 0 and by_act < T:
                            shape = [P, T - by_act, P]
                            V.tensor_tensor(near_onehot[:, q, by_act:T, :], count[:, 0:P].unsqueeze(1).to_broadcast(shape),
                                            code[:, tiles_of(b, by_act)].unsqueeze(2).to_broadcast(shape), ALU.is_equal)
                        if following:
                            look_up(b + 2, q, turn + 1, -(-k * lookups // gaps), -(-(k + 1) * lookups // gaps))

                    def link(ins, k):
                        near.mark(ins)
                        value = near.value()
                        some(k)
                        dve.wait_ge(near.sem, value)

                    by_dma, n = BY_DMA[layer][q], PICKS[layer][q]
                    now = b + (layer * BATCHES + 1)
                    dve.wait_ge(picked, now)
                    mask = masked[:, 0:n * GD]
                    V.tensor_tensor(mask.rearrange("p (t a d) -> p t a d", t=n, a=GROUPS),
                                    picked_rows(layer, q).rearrange("p t (a d) -> p t a d", a=GROUPS),
                                    in_group[:, tiles_of(b, by_dma), :].unsqueeze(3).to_broadcast([P, n, GROUPS, D]),
                                    ALU.mult).then_inc(picked_taken, 1)
                    some(0)
                    dve.wait_ge(picked_taken, now + 2)
                    row = gathered_rows[:, q, by_dma:T, 0:D] if layer < 2 else source_x[:, 0:n, :]
                    link(V.tensor_reduce(row, mask.rearrange("p (t a d) -> p t d a", t=n, a=GROUPS), AX.X, ALU.add), 1)
                    used = 2
                    if layer >= 2:
                        source, source_t = source_x[:, 0:n, :], source_tmp[:, 0:n, :]
                        prod, mats = product[:, 0:n * D * D], matrices[:, 0:n * D * D]
                        if layer == 3:
                            near.mark(V.tensor_tensor(source_t, source,
                                                      score_wide[:, 0, :].unsqueeze(1).to_broadcast([P, n, D]), ALU.mult))
                        dve.wait_ge(matrices_ready, b + ((layer - 2) * BATCHES + 1))
                        V.tensor_tensor(prod.rearrange("p (t o i) -> p t o i", t=n, o=D),
                                        mats.rearrange("p (t o i) -> p t o i", t=n, o=D),
                                        source.unsqueeze(2).to_broadcast([P, n, D, D]), ALU.mult).then_inc(matrices_taken, 1)
                        some(2)
                        dve.wait_ge(matrices_taken, b + ((layer - 2) * BATCHES + 2))
                        if layer == 3:
                            near.mark(V.tensor_reduce(gathered_rows[:, q, by_dma:T, D], source_t, AX.X, ALU.add))
                        msg = message32(layer, q)
                        link(V.tensor_reduce(msg[:, by_dma:T, 0:D],
                                             prod.rearrange("p (t o i) -> p t o i", t=n, o=D), AX.X, ALU.add), 3)
                        dve.wait_ge(gathered[layer][q], turn * (16 * by_dma) + 16 * by_dma)
                        if layer == 3:
                            near.mark(V.tensor_tensor(score[:], gathered_rows[:, q, :, D], attr_score[:, tiles_of(b)], ALU.add))
                        link(V.tensor_copy(msg[:, 0:by_dma, 0:D], gathered_rows[:, q, 0:by_dma, 0:D]), gaps - 1)
                        dve.sem_inc(taken, 1)
                        if layer == 2:
                            dve.sem_inc(moving_ready, 1)
                        else:
                            V.tensor_tensor(msg[:, :, D:2 * D], msg[:, :, 0:D], score[:].unsqueeze(2).to_broadcast([P, T, D]),
                                            ALU.mult).then_inc(moving_ready, 1)
                        return
                    cut_message(layer, b, q, lambda: dve.wait_ge(gathered[layer][q], turn * (16 * by_dma) + 16 * by_dma), near,
                                lambda k: some(used + k), moving_ready)

                def add_window(b, q, turn):
                    dve.wait_ge(added, b + (layer * BATCHES + 3))
                    at = bass.ds(turn * STEP2 + q * STEP1, P)
                    V.tensor_tensor(spread[0:c, at], spread[0:c, at], window_sums(q, c), ALU.add).then_inc(window_taken, 1)

                part = [xparts[:, :, k, :].rearrange("p j (a d) -> p j a d", a=GROUPS) for k in range(PARTS)]
                link(V.tensor_copy(part[0], by_group(x)))
                link(V.tensor_tensor(by_group(square[:]), by_group(x), part[0], ALU.subtract))
                link(V.tensor_copy(part[1], by_group(square[:])))
                link(V.tensor_tensor(part[2], by_group(square[:]), part[1], ALU.subtract))
                if layer == 0:
                    count_column()
                look_up(0, 0, 0)
                look_up(1, 1, 0)
                if layer == 2:
                    dve.wait_ge(table2_saved, 16 * XPOSE)
                near.mark(V.memset(spread[:], 0.0))
                send(0, 0, 0, True)
                send(1, 1, 0, True)

                def turn(i):
                    for q in range(2):
                        add_window(i * 2 + q, q, i)
                        send(i * 2 + 2 + q, q, i + 1, True)

                turn.layer_kind = ("near", layer)
                loop_of(near, TURNS - 2, turn)
                for q in range(2):
                    add_window(BATCHES - 4 + q, q, TURNS - 2)
                    send(BATCHES - 2 + q, q, TURNS - 1, False)
                add_window(BATCHES - 2, 0, TURNS - 1)
                dve.wait_ge(window_taken, (layer + 1) * BATCHES + 1)
                add_window(BATCHES - 1, 1, TURNS - 1)
                dve.wait_ge(window_taken, (layer + 1) * BATCHES + 2)
                dve.sem_inc(spread_ready, 1)
                own_scores(CHUNKS[layer], near)
                dve.wait_ge(sums_ready, layer + 1)
                def by_bank(t):
                    return t.rearrange("p (b h) d -> p b h d", b=5)

                back = turned(c)
                link(V.tensor_copy(by_bank(agg[:]), back[:, :, :, 0:D]))
                if layer < 2:
                    for k in range(1, PARTS):
                        link(V.tensor_tensor(by_bank(agg[:]), by_bank(agg[:]), back[:, :, :, k * D:(k + 1) * D], ALU.add))
                if layer == 0:
                    link(V.tensor_copy(inv_count[:].rearrange("p (b h) -> p b h", b=5), back[:, :, :, c - 1]))
                if layer == 3:
                    link(V.tensor_copy(by_bank(agg2[:]), back[:, :, :, D:2 * D]))
                dve.sem_inc(sums_taken, 1)

            marks_of = {("far", 0): 10, ("far", 1): 8, ("far", 2): 8, ("far", 3): 14,
                        ("near", 0): 10, ("near", 1): 8, ("near", 2): 6, ("near", 3): 12}

            def scatter(layer):
                with dve.If_eq(is_far, 0):
                    near_scatter(layer)
                with dve.Else():
                    far_scatter(layer)

            def wide(t, n=D):
                return t.unsqueeze(1).to_broadcast([P, HI, n])

            def each(t):
                return t.unsqueeze(2).to_broadcast([P, HI, D])

            def norm(layer, ready):
                link(V.tensor_reduce(mean[:], y[:], AX.X, ALU.add))
                link(V.tensor_scalar(mean[:], mean[:], 1.0 / D, None, ALU.mult))
                link(V.tensor_tensor(y[:], y[:], each(mean[:]), ALU.subtract))
                link(V.tensor_tensor(square[:], y[:], y[:], ALU.mult))
                V.tensor_reduce(var[:], square[:], AX.X, ALU.add).then_inc(var_ready, 1)
                dve.wait_ge(std_ready, layer + 1)
                link(V.reciprocal(mean[:], var[:]))
                link(V.tensor_tensor(x, y[:], each(mean[:]), ALU.mult))
                if ready:
                    dve.sem_inc(cat_ready, 1)

            scatter(0)
            link(V.tensor_scalar(inv_count[:], inv_count[:], 1.0, None, ALU.max))
            link(V.reciprocal(inv_count[:], inv_count[:]))
            link(V.tensor_tensor(agg[:], agg[:], wide(l0_w[:]), ALU.mult))
            link(V.scalar_tensor_tensor(agg[:], x, l0_self[:], agg[:], ALU.mult, ALU.add))
            link(V.tensor_tensor(agg[:], agg[:], x, ALU.add))
            link(V.tensor_scalar(agg[:], agg[:], 0.0, 1.0, ALU.max, ALU.min))
            link(V.tensor_tensor(y[:], agg[:], x, ALU.add))
            norm(0, 1)

            scatter(1)
            link(V.tensor_tensor(cat[:, :, D:2 * D], agg[:], each(inv_count[:]), ALU.mult))
            dve.sem_inc(cat_ready, 1)
            link(V.tensor_tensor(agg[:], x, wide(l1_b[:]), ALU.add))
            dve.wait_ge(by_rel_loaded, 16)
            for k, n in enumerate((PARTS * TYPES, RELS)):
                raw = type_raw[k][:] if k == 0 else type_raw[k][:].rearrange("r (i o) -> r o i", i=D)
                left = type_rest[0:n, :]
                if k == 1:
                    left = left.rearrange("r (o i) -> r o i", i=D)
                part = [type_parts[k][:, m, :] if k == 0 else type_parts[k][:, m, :].rearrange("r (o i) -> r o i", i=D)
                        for m in range(PARTS)]
                link(V.tensor_copy(part[0], raw))
                link(V.tensor_tensor(left, raw, part[0], ALU.subtract))
                link(V.tensor_copy(part[1], left))
                link(V.tensor_tensor(part[2], left, part[1], ALU.subtract))
            own_scores(range(2, 3), step)
            link(V.tensor_scalar(type_rest[0:PARTS * TYPES, :], type_parts[0][:, 0, :], own_part[0:PARTS * TYPES, 0:1], None, ALU.mult))
            for m in range(1, PARTS):
                to = type_rest[0:PARTS * TYPES, :] if m < PARTS - 1 else emb_stack[:]
                link(V.scalar_tensor_tensor(to, type_parts[0][:, m, :], own_part[0:PARTS * TYPES, m:m + 1],
                                            type_rest[0:PARTS * TYPES, :], ALU.mult, ALU.add))
            empty("l1_linear", lambda b: V.tensor_tensor(y[:].rearrange("p h d -> p (h d)"), b[:, 0:HI * D],
                                                         agg[:].rearrange("p h d -> p (h d)"), ALU.add))
            norm(1, 3)

            own_scores(range(3, 7), step)

            scatter(2)
            link(V.tensor_copy(cat[:, :, D:2 * D], agg[:]))
            dve.sem_inc(cat_ready, 1)
            dve.wait_ge(wrel_loaded, 16)
            link(V.tensor_copy(wrel[:, :, D:ROW3], score_w[:].unsqueeze(1).to_broadcast([D, RELS, 1])))
            whole = wrel[:].rearrange("i r o -> i (r o)")
            link(V.tensor_copy(wrel_split[:, 0, :], whole))
            link(V.tensor_tensor(whole, whole, wrel_split[:, 0, :], ALU.subtract))
            link(V.tensor_copy(wrel_split[:, 1, :], whole))
            link(V.tensor_tensor(wrel_split[:, 2, :], whole, wrel_split[:, 1, :], ALU.subtract))
            dve.sem_inc(wrel_ready, 1)
            for g in range(GATES):
                n = min(8, HI - 8 * g)
                empty(f"l2_gates{g}", lambda b: V.tensor_tensor(
                    gates[:, 8 * g:8 * g + n, :], b[:, 0:n * 4 * D].rearrange("p (h c) -> p h c", h=n),
                    gate_b[:].unsqueeze(1).to_broadcast([P, n, 4 * D]), ALU.add))
            dve.sem_inc(gate_in, 1)
            dve.wait_ge(gate_out, 1)
            link(V.tensor_scalar(gates[:, :, 0:2 * D], gates[:, :, 0:2 * D], 0.5, 0.5, ALU.mult, ALU.add))
            link(V.tensor_tensor(agg[:], gates[:, :, 0:D], gates[:, :, 3 * D:4 * D], ALU.mult))
            V.tensor_tensor(gates[:, :, 2 * D:3 * D], gates[:, :, 2 * D:3 * D], agg[:], ALU.add).then_inc(gate_in, 1)
            dve.wait_ge(gate_out, 2)
            new = gates[:, :, 2 * D:3 * D]
            link(V.tensor_tensor(agg[:], x, new, ALU.subtract))
            link(V.tensor_tensor(agg[:], agg[:], gates[:, :, D:2 * D], ALU.mult))
            link(V.tensor_tensor(agg[:], agg[:], new, ALU.add))
            link(V.tensor_tensor(y[:], agg[:], x, ALU.add))
            norm(2, None)
            first = x_split[:, :, 0, :].rearrange("p h (k d) -> p h k d", k=PARTS)
            link(V.tensor_copy(first[:, :, 0, :], x))
            link(V.tensor_tensor(square[:], x, first[:, :, 0, :], ALU.subtract))
            link(V.tensor_copy(first[:, :, 1, :], square[:]))
            link(V.tensor_tensor(first[:, :, 2, :], square[:], first[:, :, 1, :], ALU.subtract))
            link(V.tensor_copy(x_split[:, :, 1, :], x_split[:, :, 0, :]))
            dve.sem_inc(cat_ready, 1)
            n = 0
            for h in range(HI):
                if h >= STAGES:
                    dve.wait_ge(table3_saved[h % STAGES], 16 * (h // STAGES))
                for c in range((h + 1) % 2, 3, 2):
                    name = f"t3_rows{h}_{c}"
                    dve.wait_ge(filled, fill_no[name] + 1)
                    n += 1
                    V.tensor_copy(table3[:, h % STAGES, c * CUT * ROW3:(c + 1) * CUT * ROW3],
                                  bank(name)[:, 0:CUT * ROW3]).then_inc(staged_dve, 1)
                    dve.wait_ge(staged_dve, n)
                    dve.sem_inc(emptied[fill_no[name] % 3], 1)

            scatter(3)
            link(V.tensor_tensor(square[:], x, wide(score_wide[:, 2, :]), ALU.mult))
            link(V.tensor_reduce(mean[:], square[:], AX.X, ALU.add))
            link(V.tensor_tensor(agg[:], agg[:], each(mean[:]), ALU.mult))
            link(V.tensor_tensor(agg[:], agg[:], agg2[:], ALU.add))
            link(V.tensor_tensor(y[:], agg[:], x, ALU.add))
            norm(3, 6)

        @block.tensor
        def _(pe):
            def start(name):
                n = fill_no[name]
                if n >= 3:
                    pe.wait_ge(emptied[n % 3], n // 3)
                return bank(name)

            def transpose(step, rows):
                for g in range(XPOSE):
                    b = start(f"{step}_xpose{g}")
                    for k, h in enumerate(four(g)):
                        last = nc.tensor.transpose(b[0:rows, k * P:(k + 1) * P], cat[:, h, 0:rows], ident[:])
                    last.then_inc(filled, 1)

            def far_scatter(layer):
                c = COLS[layer]
                for b in range(BANKS[layer]):
                    nc.tensor.matmul(sums[:, 512 * b:512 * b + 512], zeros[:, 0:P], zeros[:], start=True, stop=False)
                with pe.Fori(0, TURNS) as i:
                    for q in range(2):
                        pe.wait_ge(moving_ready, i * 2 + (layer * BATCHES + q + 1))
                        mov = moving[:, q, 0:T * GROUPS * c].rearrange("p (t c) -> p t c", t=T)
                        for t in range(T):
                            for j in range(BLOCKS):
                                last = nc.tensor.matmul(sums_of(layer)[:, j, 0:GROUPS * c], onehot[:, q, t, j * P:(j + 1) * P],
                                                        mov[:, t, :], start=False, stop=False, skip_group_check=True)
                        last.then_inc(added, 1)
                for b in range(BANKS[layer]):
                    last = nc.tensor.matmul(sums[:, 512 * b:512 * b + 512], zeros[:, 0:P], zeros[:], start=False, stop=True)
                last.then_inc(sums_ready, 1)

            def near_scatter(layer):
                c = near_width(layer)

                def pick(b, q):
                    pe.wait_ge(lookup_ready, b + (layer * BATCHES + 1))
                    pe.wait_ge(picked_taken, b + (layer * BATCHES + 1))
                    for t in range(PICKS[layer][q]):
                        for j in range(BLOCKS):
                            for k in range(PARTS):
                                last = nc.tensor.matmul(picked_rows(layer, q)[:, t, :], lookup_of(layer)[:, q, j, t * P:(t + 1) * P], xparts[:, j, k, :],
                                                        start=j == 0 and k == 0, stop=j == BLOCKS - 1 and k == PARTS - 1)
                    last.then_inc(picked, 1)

                def pick_matrices(b, q):
                    if layer < 2:
                        return
                    pe.wait_ge(matrices_taken, b + ((layer - 2) * BATCHES + 1))
                    for t in range(PICKS[layer][q]):
                        if layer == 2:
                            last = nc.tensor.matmul(matrices[:, t * D * D:(t + 1) * D * D],
                                                    type_lookup[0:PARTS * TYPES, q, t * P:(t + 1) * P], emb_stack[:],
                                                    start=True, stop=True)
                            continue
                        for k in range(PARTS):
                            last = nc.tensor.matmul(matrices[:, t * D * D:(t + 1) * D * D], type_lookup[0:RELS, q, t * P:(t + 1) * P],
                                                    type_parts[1][:, k, :], start=k == 0, stop=k == PARTS - 1)
                    last.then_inc(matrices_ready, 1)

                def add(b, q):
                    pe.wait_ge(windows_ready, b + (layer * BATCHES + 1))
                    pe.wait_ge(window_taken, b + (layer * BATCHES + 1))
                    pe.wait_ge(moving_ready, b + (layer * BATCHES + 1))
                    for t in range(T):
                        msg = parts[:, q, t * c:(t + 1) * c] if layer < 2 else message32(layer, q)[:, t, :]
                        last = nc.tensor.matmul(window_sums(q, c), msg, windows_of(layer)[:, q, t, :],
                                                start=t == 0, stop=t == T - 1)
                    last.then_inc(added, 1)

                pick(0, 0)
                pick_matrices(0, 0)
                pick(1, 1)
                with pe.Fori(0, TURNS - 1) as i:
                    for q in range(2):
                        pick_matrices(i * 2 + 1 + q, 1 - q)
                        pick(i * 2 + 2 + q, q)
                        add(i * 2 + q, q)
                pick_matrices(BATCHES - 1, 1)
                add(BATCHES - 2, 0)
                add(BATCHES - 1, 1)
                pe.wait_ge(spread_ready, layer + 1)
                for h in range(HI):
                    piece = spread[0:c, MARGIN + h * P:MARGIN + (h + 1) * P]
                    last = nc.tensor.transpose(turned(c)[:, h // 5, h % 5, :], piece, ident[0:c, 0:c])
                last.then_inc(sums_ready, 1)

            def scatter(layer):
                if layer:
                    pe.wait_ge(sums_taken, layer)
                with pe.If_eq(is_far, 0):
                    near_scatter(layer)
                with pe.Else():
                    far_scatter(layer)

            pe.wait_ge(const_done, 1)
            pe.sem_inc(added, 2)
            pe.wait_ge(loaded["weights"], 16 * 18)
            nc.tensor.matmul(start("wrel")[0:RELS, 0:D * D], compT[:], bases[:].rearrange("b i o -> b (i o)"),
                             start=True, stop=True).then_inc(filled, 1)
            pe.wait_ge(bounds_ready, 1)
            nc.tensor.matmul(start("bounds")[0:1, 0:1], bounds[:, 1:2], ones[:], start=True, stop=True).then_inc(filled, 1)
            def codes(k, numbers):
                for g in range(2):
                    b = start(f"codes{k}_{g}")
                    for m, t in enumerate(range(4 * g * P, min(4 * (g + 1) * P, TILES), P)):
                        n = min(P, TILES - t)
                        last = nc.tensor.transpose(b[0:n, m * P:(m + 1) * P], numbers[:, t:t + n], ident[:])
                    last.then_inc(filled, 1)

            pe.wait_ge(edges_ready[2], 1)
            codes(0, src_code)
            nc.tensor.matmul(start("score_w")[0:D, 0:1], ws[:], waT[:, 0:1], start=True, stop=True).then_inc(filled, 1)
            b = start("score_wide")
            pe.wait_ge(wide_ready, 1)
            for k in range(3):
                last = nc.tensor.matmul(b[:, k * D:(k + 1) * D], wa_wide[:, k, :], ws[:], start=True, stop=True)
            last.then_inc(filled, 1)

            pe.wait_ge(types_ready, 1)
            codes(1, type_f[0])
            codes(2, type_f[1])
            pe.wait_ge(far_ready, 1)
            is_far = pe.alloc_register("is_far_pe")
            pe.reg_load(is_far, far[0:1, 0:1])
            scatter(0)
            scatter(1)
            pe.wait_ge(cat_ready, 2)
            transpose("l1", 2 * D)
            b = start("l1_linear")
            pe.wait_ge(catT_ready, XPOSE)
            for h in range(HI):
                last = nc.tensor.matmul(b[:, h * D:(h + 1) * D], catT[0:2 * D, h * P:(h + 1) * P], l1_w[:], start=True, stop=True)
            last.then_inc(filled, 1)
            pe.wait_ge(cat_ready, 3)
            transpose("t2", D)
            pe.wait_ge(catT_ready, 2 * XPOSE)
            for g in range(XPOSE):
                b = start(f"t2_rows{g}")
                for k, h in enumerate(four(g)):
                    last = nc.tensor.matmul(b[:, k * P:(k + 1) * P], catT[0:D, h * P:(h + 1) * P],
                                            emb[:].rearrange("i t o -> i (t o)"), start=True, stop=True)
                last.then_inc(filled, 1)
            scatter(2)
            pe.wait_ge(cat_ready, 4)
            transpose("l2", 2 * D)
            pe.wait_ge(catT_ready, 3 * XPOSE)
            for g in range(GATES):
                b = start(f"l2_gates{g}")
                for k, h in enumerate(range(8 * g, min(8 * g + 8, HI))):
                    last = nc.tensor.matmul(b[:, k * 4 * D:(k + 1) * 4 * D], catT[0:2 * D, h * P:(h + 1) * P], gate_w[:],
                                            start=True, stop=True)
                last.then_inc(filled, 1)
            pe.wait_ge(cat_ready, 5)
            for g in range(XPOSE):
                b = start(f"t3_xpose{g}")
                for k, h in enumerate(four(g)):
                    last = nc.tensor.matmul(b[0:2 * PARTS * D, k * P:(k + 1) * P], x_split[:, h, :, :].rearrange("p r c -> p (r c)"),
                                            ident_bf[:], start=True, stop=True)
                last.then_inc(filled, 1)
            pe.wait_ge(catT_ready, 4 * XPOSE)
            pe.wait_ge(wrel_stacked, 16 * 3 * PARTS)
            for h in range(HI):
                for c in range(3):
                    b = start(f"t3_rows{h}_{c}")
                    cols = slice(c * CUT * ROW3, (c + 1) * CUT * ROW3)
                    nc.tensor.matmul(b[:, 0:CUT * ROW3], x_splitT[0:2 * PARTS * D, h * P:(h + 1) * P], w_parts12[:, cols],
                                     start=True, stop=False)
                    nc.tensor.matmul(b[:, 0:CUT * ROW3], x_splitT[0:PARTS * D, h * P:(h + 1) * P], w_part3[:, cols],
                                     start=False, stop=True).then_inc(filled, 1)
            scatter(3)


def kernel(**inputs):
    import numpy as _np
    import concourse.bacc as _bacc
    from concourse import mybir as _mybir
    from concourse.bass_utils import run_bass_kernel_spmd as _run

    nc = _bacc.Bacc("TRN2", target_bir_lowering=False, num_devices=1)
    arrays, given = {}, {}

    def give(name, x):
        x = _np.ascontiguousarray(x)
        arrays[f"in_{name}"] = x
        given[name] = nc.dram_tensor(f"in_{name}", x.shape, _mybir.dt.from_np(x.dtype), kind="ExternalInput").ap()

    for name in ("src", "dst", "edge_type_8", "edge_type_90", "edge_weight", "edge_attr_16"):
        edges = _np.asarray(inputs[name])
        whole, rest = edges[:FULL * P], edges[FULL * P:]
        whole = _np.reshape(whole, (FULL // T, P, T * (edges.size // EDGES)))
        give(name, _np.reshape(_np.transpose(whole, (1, 0, 2)), (P, -1)))
        give(name + "_tail", _np.reshape(rest, (-1,)))
    for name in ("x", "L0_gnn_weight", "L1_gnn_b_l", "L2_gnn_b_ih", "L2_gnn_b_hh", "L2_gnn_edge_emb", "L3_gnn_Ws"):
        give(name, inputs[name])
    give("L0_gnn_self_loop_weight", _np.reshape(inputs["L0_gnn_self_loop_weight"], (1,)))
    give("W_lT", _np.transpose(inputs["L1_gnn_W_l"]))
    give("W_rT", _np.transpose(inputs["L1_gnn_W_r"]))
    give("w_ihT", _np.transpose(inputs["L2_gnn_w_ih"]))
    give("w_hhT", _np.transpose(inputs["L2_gnn_w_hh"]))
    give("L2_gnn_edge_embT", _np.transpose(_np.reshape(inputs["L2_gnn_edge_emb"], (TYPES, D, D)), (2, 0, 1)))
    give("WaT", _np.transpose(_np.reshape(inputs["L3_gnn_Wa"], (3, D))))
    give("w_compT", _np.transpose(inputs["L3_gnn_w_comp"]))
    give("bases", _np.transpose(_np.reshape(inputs["L3_gnn_weight"], (D, BASES, D)), (1, 0, 2)))
    f32 = _mybir.dt.float32
    tables = {
        "wrel": nc.dram_tensor("wrel_flat", (RELS * D * D,), f32).ap(),
        "codes": nc.dram_tensor("edge_codes", (3 * TILES * P,), _mybir.dt.float16).ap(),
        "rows1": nc.dram_tensor("rows1", (PADDED, D), f32).ap(),
        "rows2": nc.dram_tensor("rows2", (PADDED * TYPES, D), f32).ap(),
        "rows3": nc.dram_tensor("rows3", (PADDED * RELS, ROW3), f32).ap(),
    }
    out = nc.dram_tensor("out_0", (NODES, D), f32, kind="ExternalOutput").ap()
    gnn_kernel(nc, given, tables, out)
    r = _run(nc, [arrays], core_ids=[0])
    return r.results[0]["out_0"]
```
